# Optimizing a Trainium2 kernel written in Bass

```python
import numpy as np
import jax
import jax.numpy as jnp

def _softmax(x, axis=-1):
    return jax.nn.softmax(x, axis=axis)

def _gelu(x):
    return jax.nn.gelu(x, approximate=True)

def _silu(x):
    return jax.nn.silu(x)

def _sigmoid(x):
    return jax.nn.sigmoid(x)

def _layernorm(x, axis=-1, eps=1e-05):
    m = jnp.mean(x, axis=axis, keepdims=True)
    v = jnp.var(x, axis=axis, keepdims=True)
    return (x - m) / jnp.sqrt(v + eps)

def _scatter_add(tgt, idx, src, axis=0):
    return tgt.at[idx].add(src)

def _segment_sum(src, seg, n):
    return jax.ops.segment_sum(src, seg, n)
kernel_name = 'mk_adaln_attn_ffn_d1_seqx_r4_5d9666'

def setup_inputs(seed: int=0):
    np.random.seed(seed)
    _w = jnp.asarray

    def _rec_inputs():
        import jax
        import jax.numpy as jnp
        _rk = jax.random.key(seed)
        x = -7.109e-05 + 0.9999 * jax.random.normal(jax.random.fold_in(_rk, 1), (32, 64, 512), jnp.float32)
        _lenS = 64 - jax.random.randint(jax.random.fold_in(_rk, 7), (32,), 0, max(1, 64 // 4) + 1, jnp.int32)
        _lenS2 = 64 - jax.random.randint(jax.random.fold_in(_rk, 8), (32,), 0, max(1, 64 // 4) + 1, jnp.int32)
        itok_B_0_7 = jax.random.randint(jax.random.fold_in(_rk, 11), (32,), 0, 8, jnp.int32)
        itok_B_1_198 = jax.random.randint(jax.random.fold_in(_rk, 12), (32,), 1, 199, jnp.int32)
        return (x, itok_B_0_7, itok_B_1_198)
    x, itok_B_0_7, itok_B_1_198 = _rec_inputs()

    def _L0_cond_setup():
        import jax, jax.numpy as jnp
        import numpy as np
        B, C, D, T, N_SUBJECTS = (128, 64, 64, 512, 8)
        key = jax.random.key(seed)
        kx, ks, kw = jax.random.split(key, 3)
        x = jax.random.normal(kx, (B, C, T), dtype=jnp.float32)
        subjects = jax.random.randint(ks, (B,), 0, N_SUBJECTS, dtype=jnp.int64)
        weights = jax.random.normal(kw, (N_SUBJECTS, C, D), dtype=jnp.float32) * (1.0 / C ** 0.5)
        return {'x': x, 'subjects': subjects, 'weights': weights}
    _L0_cond_all = _L0_cond_setup()
    _L0_cond_in = {k: v for k, v in _L0_cond_all.items() if k in ('weights',)}
    del _L0_cond_all

    def _L0_attn_setup():
        import jax, jax.numpy as jnp
        import numpy as np
        H = 16
        KVH = 4
        D = 128
        HID = 512
        EPS = 1e-06
        GROUPS = H // KVH

        def elu_plus_one(x):
            return jax.nn.elu(x) + 1.0

        def _repeat_kv(x, b, s):
            x = x.reshape(b, s, KVH, 1, D)
            x = jnp.broadcast_to(x, (b, s, KVH, GROUPS, D))
            return x.reshape(b, s, H * D)

        def _split_heads(x, b, s, nh):
            return x.reshape(b, s, nh, D).transpose(0, 2, 1, 3)
        key = jax.random.key(seed)
        ks = jax.random.split(key, 8)
        s = 0.02
        return {'hidden_states': jax.random.normal(ks[0], (2, 1024, HID), jnp.float32), 'Wq': jax.random.normal(ks[1], (H * D, HID), jnp.float32) * s, 'bq': jnp.zeros((H * D,), jnp.float32), 'Wk': jax.random.normal(ks[2], (KVH * D, HID), jnp.float32) * s, 'bk': jnp.zeros((KVH * D,), jnp.float32), 'Wv': jax.random.normal(ks[3], (KVH * D, HID), jnp.float32) * s, 'bv': jnp.zeros((KVH * D,), jnp.float32), 'Wo': jax.random.normal(ks[4], (HID, H * D), jnp.float32) * s}
    _L0_attn_all = _L0_attn_setup()
    _L0_attn_in = {k: v for k, v in _L0_attn_all.items() if k in ('Wq', 'bq', 'Wk', 'bk', 'Wv', 'bv', 'Wo')}
    del _L0_attn_all

    def _L0_cond2_setup():
        import jax, jax.numpy as jnp
        import numpy as np
        B, C, T = (128, 64, 512)
        S, D = (200, 64)
        key = jax.random.key(seed)
        k1, k2, k3 = jax.random.split(key, 3)
        x = jax.random.normal(k1, (B, C, T), dtype=jnp.float32)
        conditions = jax.random.randint(k2, (B,), 0, S, dtype=jnp.int64)
        weights = jax.random.normal(k3, (S, C, D), dtype=jnp.float32) / jnp.sqrt(jnp.float32(C))
        return {'x': x, 'conditions': conditions, 'weights': weights}
    _L0_cond2_all = _L0_cond2_setup()
    _L0_cond2_in = {k: v for k, v in _L0_cond2_all.items() if k in ('weights',)}
    del _L0_cond2_all

    def _L0_ffn_setup():
        import jax, jax.numpy as jnp
        import numpy as np
        N_BLOCKS = 16
        BLOCK_SIZE = 128
        TOP_K = N_BLOCKS // 4
        key = jax.random.key(seed)
        k1, k2, k3, k4, k5 = jax.random.split(key, 5)
        in_f, out_f = (512, 2048)
        x = jax.random.normal(k1, (2, 1024, in_f), dtype=jnp.float32)
        Wr = jax.random.normal(k2, (N_BLOCKS, in_f), dtype=jnp.float32) * in_f ** (-0.5)
        br = jnp.zeros((N_BLOCKS,), dtype=jnp.float32)
        W1 = jax.random.normal(k3, (out_f, in_f), dtype=jnp.float32) * in_f ** (-0.5)
        W2 = jax.random.normal(k4, (in_f, out_f), dtype=jnp.float32) * out_f ** (-0.5)
        return {'x': x, 'Wr': Wr, 'br': br, 'W1': W1, 'W2': W2}
    _L0_ffn_all = _L0_ffn_setup()
    _L0_ffn_in = {k: v for k, v in _L0_ffn_all.items() if k in ('Wr', 'br', 'W1', 'W2')}
    del _L0_ffn_all
    return {'x': x, 'itok_B_0_7': itok_B_0_7, 'itok_B_1_198': itok_B_1_198, 'L0_cond_weights': _L0_cond_in['weights'], 'L0_attn_Wq': _L0_attn_in['Wq'], 'L0_attn_bq': _L0_attn_in['bq'], 'L0_attn_Wk': _L0_attn_in['Wk'], 'L0_attn_bk': _L0_attn_in['bk'], 'L0_attn_Wv': _L0_attn_in['Wv'], 'L0_attn_bv': _L0_attn_in['bv'], 'L0_attn_Wo': _L0_attn_in['Wo'], 'L0_cond2_weights': _L0_cond2_in['weights'], 'L0_ffn_Wr': _L0_ffn_in['Wr'], 'L0_ffn_br': _L0_ffn_in['br'], 'L0_ffn_W1': _L0_ffn_in['W1'], 'L0_ffn_W2': _L0_ffn_in['W2']}

def reference(x, itok_B_0_7, itok_B_1_198, L0_cond_weights, L0_attn_Wq, L0_attn_bq, L0_attn_Wk, L0_attn_bk, L0_attn_Wv, L0_attn_bv, L0_attn_Wo, L0_cond2_weights, L0_ffn_Wr, L0_ffn_br, L0_ffn_W1, L0_ffn_W2):
    import jax
    import jax.numpy as jnp

    def _L0_cond_ref(x, subjects, weights):
        import jax, jax.numpy as jnp
        import numpy as np
        B, C, D, T, N_SUBJECTS = (128, 64, 64, 512, 8)
        w = weights[subjects]
        out = jnp.einsum('bct,bcd->bdt', x, w)
        return out

    def _L0_attn_ref(hidden_states, Wq, bq, Wk, bk, Wv, bv, Wo):
        import jax, jax.numpy as jnp
        import numpy as np
        H = 16
        KVH = 4
        D = 128
        HID = 512
        EPS = 1e-06
        GROUPS = H // KVH

        def elu_plus_one(x):
            return jax.nn.elu(x) + 1.0

        def _repeat_kv(x, b, s):
            x = x.reshape(b, s, KVH, 1, D)
            x = jnp.broadcast_to(x, (b, s, KVH, GROUPS, D))
            return x.reshape(b, s, H * D)

        def _split_heads(x, b, s, nh):
            return x.reshape(b, s, nh, D).transpose(0, 2, 1, 3)
        b, s, _ = hidden_states.shape
        q = hidden_states @ Wq.T + bq
        k = hidden_states @ Wk.T + bk
        v = hidden_states @ Wv.T + bv
        k = _repeat_kv(k, b, s)
        v = _repeat_kv(v, b, s)
        q = _split_heads(q, b, s, H)
        k = _split_heads(k, b, s, H)
        v = _split_heads(v, b, s, H)
        sq = elu_plus_one(q)
        sk = elu_plus_one(k)
        kv = jnp.einsum('bhsd,bhse->bhde', sk, v)
        qkv = jnp.einsum('bhsd,bhde->bhse', sq, kv)
        k_sum = sk.sum(axis=2)
        norm = jnp.einsum('bhsd,bhd->bhs', sq, k_sum)
        attn = qkv / (norm[..., None] + EPS)
        attn = attn.transpose(0, 2, 1, 3).reshape(b, s, H * D)
        return attn @ Wo.T

    def _L0_cond2_ref(x, conditions, weights):
        import jax, jax.numpy as jnp
        import numpy as np
        B, C, T = (128, 64, 512)
        S, D = (200, 64)
        w = weights[conditions]
        return jnp.einsum('bct,bcd->bdt', x, w)

    def _L0_ffn_ref(x, Wr, br, W1, W2):
        import jax, jax.numpy as jnp
        import numpy as np
        N_BLOCKS = 16
        BLOCK_SIZE = 128
        TOP_K = N_BLOCKS // 4
        x_shape = x.shape
        in_f = x_shape[-1]
        xf = x.reshape(-1, in_f)
        n = xf.shape[0]
        prob = jax.nn.softmax(xf @ Wr.T + br, axis=-1)
        _, idx = jax.lax.top_k(prob, TOP_K)
        mask = jnp.zeros((n, N_BLOCKS), dtype=xf.dtype)
        mask = mask.at[jnp.arange(n)[:, None], idx].set(1.0)
        W1b = W1.reshape(N_BLOCKS, BLOCK_SIZE, in_f)
        h = jnp.einsum('nf,ibf->nib', xf, W1b)
        h = jax.nn.gelu(h, approximate=False) * mask[:, :, None]
        W2b = W2.reshape(in_f, N_BLOCKS, BLOCK_SIZE)
        y = jnp.einsum('nib,fib->nf', h, W2b)
        return y.reshape(x_shape)
    x = x + _L0_attn_ref(_L0_cond_ref(x, itok_B_0_7, L0_cond_weights), L0_attn_Wq, L0_attn_bq, L0_attn_Wk, L0_attn_bk, L0_attn_Wv, L0_attn_bv, L0_attn_Wo)
    x = x + _L0_ffn_ref(_L0_cond2_ref(x, itok_B_1_198, L0_cond2_weights), L0_ffn_Wr, L0_ffn_br, L0_ffn_W1, L0_ffn_W2)
    return x

_drawn_inputs = setup_inputs


def setup_inputs(seed=0):
    import zlib

    import numpy as np

    out = dict(_drawn_inputs(seed))
    spreads = {'L0_attn_bq': (0.0, 0.8),
     'L0_attn_bk': (0.0, 0.8),
     'L0_attn_bv': (0.0, 0.1),
     'L0_ffn_br': (0.0, 0.1)}
    factors = {'L0_attn_Wq': 5.856, 'L0_attn_Wk': 4.969}
    for name, (base, spread) in spreads.items():
        noise = np.random.default_rng([zlib.crc32(name.encode()), seed]).standard_normal(out[name].shape)
        drawn = base * np.exp(spread * noise) if base else spread * noise
        out[name] = jnp.asarray(drawn.astype(out[name].dtype))
    for name, factor in factors.items():
        out[name] = (out[name] * factor).astype(out[name].dtype)
    return out
```

```python
import concourse.bass as bass
from concourse import mybir
from contextlib import ExitStack

F32 = mybir.dt.float32
F16 = mybir.dt.float16
I32 = mybir.dt.int32
U32 = mybir.dt.uint32
ALU = mybir.AluOpType
ACT = mybir.ActivationFunctionType
AX = mybir.AxisListType

B, C, T = 32, 64, 512
H, KVH, D = 16, 4, 128
GQ = H // KVH
NB, TOPK = 16, 4
KC = T // 128
GB = 8
NG = B // GB
TOK = GB * C
NP = GB // 2
DV = D + 1
WS = 32.0
AS = 16.0
EPS = 1e-6
UNDERFLOW = -104.0
SP_, SQ_, SA_, SF_ = NP, H + NP, KVH * NP, NP + 6 * NP
A_CR = 8


def adaln_attn_ffn(nc, x_d, i1_d, i2_d, cw_d, cw2_d, wq_d, wk_d, wv_d, wo_d, bq_d, bk_d, bv_d,
                   wr_d, br_d, w1_d, w2_d, x1_d, out_d):
    ctx = ExitStack()
    with ctx:
        def sb(name, shape, dt):
            return ctx.enter_context(nc.sbuf_tensor(name, shape, dt))

        def pb(name):
            return ctx.enter_context(nc.psum_tensor(name, [128, 512], F32))

        def sem(name):
            return ctx.enter_context(nc.semaphore(name))

        wa = sb("wa", [128, 2, KC, H * D], F16)
        wb = sb("wb", [128, 2, H, T], F16)
        wk = sb("wk", [128, 2, KC, KVH * D], F16)
        wv = sb("wv", [128, 2, KC, KVH * D], F16)
        wr = sb("wr", [128, 2, KC, NB], F16)
        wr32 = sb("wr32", [128, KC, NB], F32)
        bq = sb("bq", [128, H], F32)
        bq1 = sb("bq1", [128, H], F32)
        bk1 = sb("bk1", [128, KVH * D], F32)
        bv = sb("bv", [128, KVH * D], F32)
        brb = sb("brb", [128, NB], F32)
        negone = sb("negone", [128, 1], F32)
        zero = sb("zero", [128, 1], F32)
        idx = sb("idx", [1, 2, B], I32)
        ident = sb("ident", [128, 128], F32)
        iota = sb("iota", [128, NB], F32)
        stage = sb("stage", [128, 2, 512], F32)
        xin = sb("xin", [128, 2, T], F32)
        xs = sb("xs", [128, 2, 2, T], F16)
        cw = sb("cw", [128, 2, 128], F32)
        cws = sb("cws", [128, 2, 2, 128], F16)
        hT = sb("hT", [128, 2, KC, TOK], F16)
        ku = sb("ku", [128, KVH * D], F32)
        kf = sb("kf", [128, KVH * D], F32)
        vf = sb("vf", [128, KVH * D], F32)
        sk = sb("sk", [128, 2, 2, KVH * D], F16)
        vs = sb("vs", [128, 2, 2, KVH, DV], F16)
        kv = sb("kv", [128, 2, GB, KVH, DV], F16)
        e = sb("e", [128, 2, TOK], F32)
        u = sb("u", [128, 2, TOK], F32)
        sq = sb("sq", [128, 2, 2, GB, GQ, C], F16)
        att = sb("att", [128, 2, 4, 128], F32)
        den = sb("den", [128, 4], F32)
        rden = sb("rden", [128, 4], F32)
        mid = sb("mid", [128, 2, H, TOK], F16)
        xres = sb("xres", [128, 2, T], F32)
        w2s = (kv[:].rearrange("p a b j d -> p (a b j d)")[:, 0:H * T].rearrange("p (h t) -> p h t", h=H),
               sq[:].rearrange("p s a b h c -> p (s a b h c)").rearrange("p (h t) -> p h t", h=H))
        stages = (stage[:, 0, :], stage[:, 1, :], kf[:], vf[:])
        wstage = mid[:].rearrange("p a h t -> p (a h t)").bitcast(F32).rearrange("p (c n) -> p c n", n=512)
        lg = sb("lg", [128, NP, NB], F32)
        mx = sb("mx", [128, NP], F32)
        top = sb("top", [128, NP, 8], F32)
        topi = sb("topi", [128, NP, 8], U32)
        topf = sb("topf", [128, NP, 8], F32)
        eq = ku[:, 0:NP * TOPK * NB].rearrange("p (a k n) -> p a k n", a=NP, k=TOPK)
        mask = sb("mask", [128, NP, NB], F32)
        pad = sb("pad", [128, 1], F32)
        maskT = sb("maskT", [NB, TOK], F16)
        sel = sb("sel", [NB, NB, 128], F16)

        Q = [pb(f"Q{i}") for i in range(2)]
        F = [pb(f"F{i}") for i in range(2)]
        M = ctx.enter_context(nc.psum_tensor("M", [128, 2, 512], F32))
        TR = [pb(f"TR{i}") for i in range(2)]

        consts_in = sem("consts_in")
        pool_consts = sem("pool_consts")
        dve_consts = sem("dve_consts")
        act_consts = sem("act_consts")
        w_in = [sem(f"w_in{i}") for i in range(16)]
        w_hi = sem("w_hi")
        w_lo = sem("w_lo")
        st_in = [sem(f"st_in{i}") for i in range(4)]
        st_hi = sem("st_hi")
        st_lo = sem("st_lo")
        x_in = [sem(f"x_in{i}") for i in range(2)]
        x_hi = sem("x_hi")
        x_lo = sem("x_lo")
        cond_done = sem("cond_done")
        hT_hi = sem("hT_hi")
        f_read = sem("f_read")
        k_done = sem("k_done")
        v_done = sem("v_done")
        k_exp = sem("k_exp")
        k_elu = sem("k_elu")
        sk_hi = sem("sk_hi")
        sk_lo = sem("sk_lo")
        vs_hi = sem("vs_hi")
        vs_lo = sem("vs_lo")
        kv_done = sem("kv_done")
        kv_hi = sem("kv_hi")
        q_done = sem("q_done")
        q_free = [sem(f"q_free{i}") for i in range(2)]
        e_ready = sem("e_ready")
        e_hi = sem("e_hi")
        e_free = sem("e_free")
        heads_free = sem("heads_free")
        m_free = sem("m_free")
        t_free = sem("t_free")
        mid_hi = sem("mid_hi")
        tr_free = sem("tr_free")
        o_free = sem("o_free")
        res_in = [sem(f"res_in{i}") for i in range(2)]
        stored = [sem(f"stored{i}") for i in range(2)]
        routed = sem("routed")
        lg_read = sem("lg_read")
        dve_own = sem("dve_own")
        masked = sem("masked")
        maskT_ps = sem("maskT_ps")
        maskT_sb = sem("maskT_sb")
        spread = sem("spread")

        def front_use(g, n):
            if isinstance(g, int):
                return SF_ * min(g, NG) + NP * max(g - NG, 0) + n
            return g + n

        CHUNKS = [(w, k, 0) for w in range(2) for k in range(KC)]
        CHUNKS += [(2, k, j) for j in range(KVH) for k in range(KC)] + [(3, h, 0) for h in range(H)]

        def chunk_at(c, part):
            w, rows, cols = CHUNKS[c]
            if w == 3:
                return wb[:, part, rows, :]
            return (wk, wv, wa)[w][:, part, rows, cols * 512:(cols + 1) * 512]

        def late_chunk_at(c, part):
            if c < 16:
                return wa[:, part, c % KC, c // KC * 512:(c // KC + 1) * 512]
            return w2s[part][:, c - 16, :]

        PASSES = ((0, 0), (0, 1), (1, 0))

        block = ctx.enter_context(nc.Block())

        @block.sync
        def _(sp):
            for q in stored:
                sp.sem_inc(q, 16)
            sp.dma_start(idx[0:1, 0, :], i1_d.rearrange("(a n) -> a n", a=1)).then_inc(consts_in, 16)
            sp.dma_start(idx[0:1, 1, :], i2_d.rearrange("(a n) -> a n", a=1)).then_inc(consts_in, 16)
            sp.dma_start(bq[:], bq_d).then_inc(consts_in, 16)
            sp.dma_start(brb[:], br_d.rearrange("(a n) -> a n", a=1).to_broadcast([128, NB])).then_inc(consts_in, 16)
            sp.dma_start(bk1[:], bk_d.rearrange("(a n) -> a n", a=1).to_broadcast([128, 512])).then_inc(consts_in, 16)
            sp.dma_start(bv[:], bv_d.rearrange("(a n) -> a n", a=1).to_broadcast([128, 512])).then_inc(consts_in, 16)
            sp.dma_start(wr32[:], wr_d.rearrange("(k p) n -> p k n", p=128)).then_inc(consts_in, 16)
            sp.wait_ge(consts_in, 112)
            sp.wait_ge(pool_consts, 4)

            def load_x(g, p, layer):
                s = p % 2
                src, w_d, n = (x_d, cw_d, 8) if layer == 0 else (x1_d, cw2_d, 200)
                t = (g - NG * layer) * GB + 2 * p
                if not (isinstance(g, int) and g == 0 and p < 2):
                    sp.wait_ge(x_lo, g * NP + p - 1)
                if layer == 1:
                    sp.wait_ge(stored[s], 16 * (2 * (g - NG) + p // 2 + 2))
                sp.dma_start(xin[:, s, :], src[bass.ds(t, 2), :, :].rearrange("b c t -> (b c) t")).then_inc(x_in[s], 16)
                for h in range(2):
                    i = sp.value_load(idx[0:1, layer, bass.ds(t + h, 1)], min_val=0, max_val=n - 1)
                    sp.dma_start(cw[64 * h:64 * h + 64, s, 64 * h:64 * h + 64],
                                 w_d[bass.ds(i, 1), :, :].rearrange("a c d -> (a c) d")).then_inc(x_in[s], 16)

            def load_res(g, p, layer):
                s = p % 2
                t = (g - NG * layer) * GB + 2 * p
                sp.wait_ge(stored[s], 16 * (2 * g + p // 2 + 1))
                sp.dma_start(xres[:, s, :], (x1_d if layer else x_d)[bass.ds(t, 2), :, :]
                             .rearrange("b c t -> (b c) t")).then_inc(res_in[s], 16)

            def store(g, p, layer):
                s = p % 2
                t = (g - NG * layer) * GB + 2 * p
                sp.wait_ge(q_free[s], (SQ_ // 2) * g + H // 2 + p // 2 + 2)
                sp.dma_start((out_d if layer else x1_d)[bass.ds(t, 2), :, :]
                             .rearrange("b c t -> (b c) t"), xres[:, s, :]).then_inc(stored[s], 16)

            def body(g, layer, nxt):
                if nxt is not None:
                    load_x(g + 1, 0, nxt)
                    load_x(g + 1, 1, nxt)
                load_res(g, 0, layer)
                load_res(g, 1, layer)
                if nxt is not None:
                    load_x(g + 1, 2, nxt)
                    load_x(g + 1, 3, nxt)
                store(g, 0, layer)
                load_res(g, 2, layer)
                store(g, 1, layer)
                load_res(g, 3, layer)
                store(g, 2, layer)
                store(g, 3, layer)

            load_x(0, 0, 0)
            load_x(0, 1, 0)
            for c, (w, rows, cols) in enumerate(CHUNKS):
                if c == 4:
                    load_x(0, 2, 0)
                if c == 8:
                    load_x(0, 3, 0)
                if c >= 16:
                    sp.wait_ge(w_lo, c - 15)
                w_d = (wk_d, wv_d, wq_d, wo_d)[w]
                sp.dma_start(wstage[:, c % 16, :], w_d[rows * 128:(rows + 1) * 128, cols * 512:(cols + 1) * 512])\
                    .then_inc(w_in[c % 16], 16)
            with sp.Fori(0, NG - 1) as g:
                body(g, 0, 0)
            body(NG - 1, 0, 1)
            with sp.Fori(NG, 2 * NG - 1) as g:
                body(g, 1, 1)
            body(2 * NG - 1, 1, None)
            for q in stored:
                sp.wait_ge(q, 16 * (4 * NG + 1))

        @block.gpsimd
        def _(pool):
            pool.memset(cw[:], 0.0).then_inc(pool_consts, 1)
            pool.memset(ident[:], 0.0).then_inc(pool_consts, 1)
            pool.memset(sel[:], 0.0).then_inc(pool_consts, 1)
            pool.iota(iota[:], pattern=[[1, NB]], base=0, channel_multiplier=0,
                      allow_small_or_imprecise_dtypes=True).then_inc(pool_consts, 1)
            pool.wait_ge(pool_consts, 4)
            pool.affine_select(out=ident[:], in_=ident[:], compare_op=ALU.not_equal, fill=1.0, base=0,
                               pattern=[[-1, 128]], channel_multiplier=1).then_inc(pool_consts, 1)
            pool.affine_select(out=sel[:], in_=sel[:], compare_op=ALU.not_equal, fill=1.0, base=0,
                               pattern=[[-1, NB], [0, 128]], channel_multiplier=1).then_inc(pool_consts, 1)

            def x_split(g, p):
                s = p % 2
                pool.wait_ge(x_hi, g * NP + p + 1)
                pool.tensor_tensor(xs[:, s, 1, :], xin[:, s, :], xs[:, s, 0, :], ALU.subtract)
                pool.tensor_tensor(cws[:, s, 1, :], cw[:, s, :], cws[:, s, 0, :], ALU.subtract).then_inc(x_lo, 1)

            def kv_split(g, p):
                s = p % 2
                pool.wait_ge(sk_hi, g * NP + p + 1)
                pool.tensor_tensor(sk[:, s, 1, :], kf[:], sk[:, s, 0, :], ALU.subtract).then_inc(sk_lo, 1)
                pool.wait_ge(vs_hi, g * NP + p + 1)
                pool.tensor_tensor(vs[:, s, 1, :, 0:D], vf[:].rearrange("p (h d) -> p h d", h=KVH),
                                   vs[:, s, 0, :, 0:D], ALU.subtract).then_inc(vs_lo, 1)

            x_split(0, 0)
            x_split(0, 1)
            x_split(0, 2)
            x_split(0, 3)
            for p in range(NP):
                kv_split(0, p)
            with pool.Fori(0, NG - 1) as g:
                for p in range(NP):
                    x_split(g + 1, p)
                for p in range(NP):
                    kv_split(g + 1, p)
            for p in range(NP):
                x_split(NG, p)
            with pool.Fori(NG, 2 * NG - 1) as g:
                for p in range(NP):
                    x_split(g + 1, p)

        @block.scalar
        def _(act):
            act.wait_ge(consts_in, 112)
            act.wait_ge(dve_consts, 3)
            nc.scalar.activation(bq1[:], bq[:], ACT.Identity, bias=1.0).then_inc(act_consts, 1)
            nc.scalar.activation(wr[:, 0, :, :], wr32[:], ACT.Copy).then_inc(act_consts, 1)

            def x_high(g, p):
                s = p % 2
                act.wait_ge(x_in[s], 48 * (2 * g + p // 2 + 1))
                if not (isinstance(g, int) and g == 0 and p < 2):
                    act.wait_ge(cond_done, g * NP + p - 1)
                nc.scalar.activation(xs[:, s, 0, :], xin[:, s, :], ACT.Copy)
                nc.scalar.activation(cws[:, s, 0, :], cw[:, s, :], ACT.Copy).then_inc(x_hi, 1)

            def cond_high(g, p):
                act.wait_ge(cond_done, g * NP + p + 1)
                if not (isinstance(g, int) and g == 0):
                    act.wait_ge(q_done, H * g)
                nc.scalar.activation(hT[:, 0, :, p * 128:(p + 1) * 128], F[p % 2][:].rearrange("p (k n) -> p k n", k=KC),
                                     ACT.Copy).then_inc(hT_hi, 1)

            def k_expo(g, p, f):
                act.wait_ge(f_read, f + 4 + 6 * p + 1)
                if not (isinstance(g, int) and g == 0 and p == 0):
                    act.wait_ge(sk_lo, g * NP + p)
                nc.scalar.activation(kf[:], ku[:], ACT.Exp, bias=negone[:]).then_inc(k_exp, 1)

            def kv_high(g, p, f):
                s = p % 2
                act.wait_ge(k_elu, g * NP + p + 1)
                if not (isinstance(g, int) and g == 0 and p < 2):
                    act.wait_ge(kv_done, 4 * (g * NP + p - 1))
                nc.scalar.activation(sk[:, s, 0, :], kf[:], ACT.Copy).then_inc(sk_hi, 1)
                act.wait_ge(f_read, f + 5 + 6 * p + 1)
                nc.scalar.activation(vs[:, s, 0, :, 0:D], vf[:].rearrange("p (h d) -> p h d", h=KVH),
                                     ACT.Copy).then_inc(vs_hi, 1)

            def kvprod_high(g, p):
                for n in range(4):
                    jj, b = n // 2, n % 2
                    act.wait_ge(kv_done, 4 * (g * NP + p) + n + 1)
                    act.wait_ge(heads_free, SA_ * g + A_CR)
                    nc.scalar.activation(kv[:, 0, 2 * p + b, 2 * jj:2 * jj + 2, :],
                                         F[b][:, 0:2 * DV].rearrange("p (j d) -> p j d", j=2), ACT.Copy).then_inc(kv_hi, 1)

            def q_read(g, h):
                s = h % 2
                act.wait_ge(q_done, H * g + h + 1)
                act.wait_ge(e_free, H * g + h + 1)
                nc.scalar.activation(e[:, s, :], Q[s][:], ACT.Exp, bias=bq[:, h:h + 1], scale=1.0 / WS)
                nc.scalar.activation(u[:, s, :], Q[s][:], ACT.Identity, bias=bq1[:, h:h + 1],
                                     scale=1.0 / WS).then_inc(q_free[s], 1)

            def q_high(g, h):
                act.wait_ge(e_ready, H * g + h + 1)
                act.wait_ge(heads_free, SA_ * g + 4 * (h // GQ) - 4 + A_CR)
                nc.scalar.activation(sq[:, (h // GQ) % 2, 0, :, h % GQ, :],
                                     e[:, h % 2, :].rearrange("p (b s) -> p b s", b=GB), ACT.Copy).then_inc(e_hi, 1)

            def mid_high(g, n):
                j, i = n // NP, n % NP
                act.wait_ge(t_free, SA_ * g + n + 3)
                act.wait_ge(o_free, NP * g + 1)
                for b in range(2):
                    last = nc.scalar.activation(
                        mid[:, 0, GQ * j:GQ * j + GQ, (2 * i + b) * C:(2 * i + b + 1) * C],
                        TR[n % 2][:, b * 256:(b + 1) * 256].rearrange("p (h s) -> p h s", h=GQ), ACT.Copy)
                last.then_inc(mid_hi, 1)

            def fetch(c):
                if c >= 32:
                    return
                if c >= 4:
                    act.wait_ge(st_lo, c - 3)
                elif c >= 2:
                    act.wait_ge((sk_lo, vs_lo)[c - 2], NP * NG)
                w_d, rows, cols = (w1_d, c % KC, c // KC) if c < 16 else (w2_d, c - 16, 0)
                act.dma_start(stages[c % 4], w_d[rows * 128:(rows + 1) * 128, cols * 512:(cols + 1) * 512])\
                    .then_inc(st_in[c % 4], 16)

            def late_high(c0, c1):
                for c in range(c0, c1):
                    fetch(c + 3)
                    act.wait_ge(st_in[c % 4], 16 * (c // 4 + 1))
                    if c == 0:
                        act.wait_ge(q_done, H * NG)
                    if c == 16:
                        act.wait_ge(heads_free, SA_ * NG + A_CR)
                    nc.scalar.activation(late_chunk_at(c, 0), stages[c % 4], ACT.Copy, scale=WS).then_inc(st_hi, 1)

            def body_a(g, nxt, f):
                if nxt == 1:
                    for c in range(3):
                        fetch(c)
                for h in range(GQ):
                    q_read(g, h)
                    if h:
                        q_high(g, h - 1)
                for j in range(1, KVH):
                    for i in range(NP):
                        q_read(g, GQ * j + i)
                        q_high(g, GQ * j + i - 1)
                        n = NP * (j - 1) + i
                        if n >= 1:
                            mid_high(g, n - 1)
                        if j == KVH - 1 and i < 2:
                            x_high(g + 1, i)
                q_high(g, H - 1)
                for i in range(NP):
                    cond_high(g + 1, i)
                    if i < 2:
                        x_high(g + 1, i + 2)
                    mid_high(g, NP * (KVH - 1) + i - 1)
                mid_high(g, NP * KVH - 1)
                if nxt == 0:
                    for p in range(NP):
                        k_expo(g + 1, p, f)
                        kv_high(g + 1, p, f)
                        kvprod_high(g + 1, p)
                else:
                    late_high(0, 8)
                    mask_high(g + 1)
                    late_high(8, 32)

            def mask_high(g):
                act.wait_ge(maskT_ps, g - NG + 1)
                if not (isinstance(g, int) and g == NG):
                    act.wait_ge(spread, NB * (g - NG))
                nc.scalar.activation(maskT[:], M[0:NB, 1, :], ACT.Copy).then_inc(maskT_sb, 1)

            def gelu_read(g, h):
                s = h % 2
                act.wait_ge(q_done, H * g + h + 1)
                act.wait_ge(e_free, H * g + h + 1)
                nc.scalar.activation(e[:, s, :], Q[s][:], ACT.Gelu, bias=zero[:], scale=1.0 / WS).then_inc(q_free[s], 1)

            def gelu_high(g, h):
                act.wait_ge(e_ready, H * g + h + 1)
                act.wait_ge(o_free, NP * g + 1)
                nc.scalar.activation(mid[:, 0, h, :], e[:, h % 2, :], ACT.Copy).then_inc(e_hi, 1)

            def body_b(g, more):
                for h in range(H):
                    gelu_read(g, h)
                    if h:
                        gelu_high(g, h - 1)
                    if more and h in (12, 13):
                        x_high(g + 1, h - 12)
                gelu_high(g, H - 1)
                if more:
                    for p in range(NP):
                        cond_high(g + 1, p)
                        if p < 2:
                            x_high(g + 1, p + 2)
                    mask_high(g + 1)

            def weight_high(c0, c1):
                for c in range(c0, c1):
                    act.wait_ge(w_in[c % 16], 16 * (c // 16 + 1))
                    nc.scalar.activation(chunk_at(c, 0), wstage[:, c % 16, :], ACT.Copy, scale=WS).then_inc(w_hi, 1)

            x_high(0, 0)
            x_high(0, 1)
            weight_high(0, 4)
            cond_high(0, 0)
            x_high(0, 2)
            cond_high(0, 1)
            x_high(0, 3)
            weight_high(4, 8)
            cond_high(0, 2)
            cond_high(0, 3)
            for p in range(NP):
                k_expo(0, p, front_use(0, 0))
                kv_high(0, p, front_use(0, 0))
                kvprod_high(0, p)
                weight_high(8 + 4 * p, 12 + 4 * p)
            weight_high(24, 40)
            with act.Fori(0, NG - 1) as g:
                body_a(g, 0, (g + 1) * SF_)
            body_a(NG - 1, 1, front_use(NG, 0))
            with act.Fori(NG, 2 * NG - 1) as g:
                body_b(g, True)
            body_b(2 * NG - 1, False)

        @block.vector
        def _(dve):
            own = [0]

            def step(ins):
                own[0] += 1
                ins.then_inc(dve_own, 1)

            for q in q_free:
                dve.sem_inc(q, 1)
            dve.sem_inc(e_free, 2)
            dve.sem_inc(m_free, 1)
            dve.sem_inc(tr_free, 2)
            nc.vector.memset(negone[:], -1.0).then_inc(dve_consts, 1)
            nc.vector.memset(zero[:], 0.0).then_inc(dve_consts, 1)
            for s in range(2):
                nc.vector.memset(vs[:, s, 0, :, D:DV], 1.0)
                last = nc.vector.memset(vs[:, s, 1, :, D:DV], 0.0)
            last.then_inc(dve_consts, 1)
            dve.wait_ge(consts_in, 112)
            nc.vector.tensor_scalar(bk1[:], bk1[:], 1.0, None, ALU.add).then_inc(dve_consts, 1)
            dve.wait_ge(act_consts, 2)
            nc.vector.tensor_tensor(wr[:, 1, :, :], wr32[:], wr[:, 0, :, :], ALU.subtract).then_inc(dve_consts, 1)
            dve.wait_ge(dve_consts, 5)

            def cond_low(g, p):
                dve.wait_ge(hT_hi, g * NP + p + 1)
                nc.vector.tensor_tensor(hT[:, 1, :, p * 128:(p + 1) * 128], F[p % 2][:].rearrange("p (k n) -> p k n", k=KC),
                                        hT[:, 0, :, p * 128:(p + 1) * 128], ALU.subtract).then_inc(f_read, 1)

            def k_bias(g, p):
                dve.wait_ge(k_done, g * NP + p + 1)
                nc.vector.scalar_tensor_tensor(out=ku[:], in0=F[0][:], scalar=1.0 / WS, in1=bk1[:],
                                               op0=ALU.mult, op1=ALU.add).then_inc(f_read, 1)

            def v_bias(g, p):
                dve.wait_ge(v_done, g * NP + p + 1)
                if not (isinstance(g, int) and g == 0 and p == 0):
                    dve.wait_ge(vs_lo, g * NP + p)
                nc.vector.scalar_tensor_tensor(out=vf[:], in0=F[1][:], scalar=1.0 / WS, in1=bv[:],
                                               op0=ALU.mult, op1=ALU.add).then_inc(f_read, 1)

            def k_max(g, p):
                dve.wait_ge(k_exp, g * NP + p + 1)
                nc.vector.scalar_tensor_tensor(out=kf[:], in0=kf[:], scalar=1.0, in1=ku[:],
                                               op0=ALU.min, op1=ALU.max).then_inc(k_elu, 1)

            def kvprod_low(g, p):
                for n in range(4):
                    jj, b = n // 2, n % 2
                    dve.wait_ge(kv_hi, 4 * (g * NP + p) + n + 1)
                    nc.vector.tensor_tensor(kv[:, 1, 2 * p + b, 2 * jj:2 * jj + 2, :],
                                            F[b][:, 0:2 * DV].rearrange("p (j d) -> p j d", j=2),
                                            kv[:, 0, 2 * p + b, 2 * jj:2 * jj + 2, :], ALU.subtract).then_inc(f_read, 1)

            def q_max(g, h):
                s = h % 2
                dve.wait_ge(q_free[s], (SQ_ // 2) * g + h // 2 + 2)
                nc.vector.scalar_tensor_tensor(out=e[:, s, :], in0=e[:, s, :], scalar=1.0, in1=u[:, s, :],
                                               op0=ALU.min, op1=ALU.max).then_inc(e_ready, 1)

            def q_low(g, h):
                dve.wait_ge(e_hi, H * g + h + 1)
                nc.vector.tensor_tensor(sq[:, (h // GQ) % 2, 1, :, h % GQ, :],
                                        e[:, h % 2, :].rearrange("p (b s) -> p b s", b=GB),
                                        sq[:, (h // GQ) % 2, 0, :, h % GQ, :], ALU.subtract).then_inc(e_free, 1)

            def normalise(g, n, at):
                dve.wait_ge(heads_free, SA_ * g + n + 1 + A_CR)
                den_ps = M[:, :, D:2 * DV:DV]
                nc.vector.tensor_scalar(den[:].rearrange("p (a b) -> p a b", a=2), den_ps, EPS, 1.0 / AS,
                                        ALU.add, ALU.mult).then_inc(dve_own, 1)
                dve.wait_ge(dve_own, at + 2 * n + 1)
                nc.vector.reciprocal(rden[:], den[:]).then_inc(dve_own, 1)
                dve.wait_ge(dve_own, at + 2 * n + 2)
                dve.wait_ge(t_free, SA_ * g + n + 1)
                nc.vector.tensor_tensor(att[:, n % 2, :, :].rearrange("p (a b) d -> p a b d", a=2),
                                        M[:, :, 0:2 * DV].rearrange("p a (b d) -> p a b d", b=2)[:, :, :, 0:D],
                                        rden[:].rearrange("p (a b) -> p a b", a=2).unsqueeze(3).to_broadcast([128, 2, 2, D]),
                                        ALU.mult).then_inc(m_free, 1)

            def mid_low(g, n):
                j, i = n // NP, n % NP
                dve.wait_ge(mid_hi, SA_ * g + n + 1)
                for b in range(2):
                    at = (slice(GQ * j, GQ * j + GQ), slice((2 * i + b) * C, (2 * i + b + 1) * C))
                    last = nc.vector.tensor_tensor(mid[:, 1, at[0], at[1]],
                                                   TR[n % 2][:, b * 256:(b + 1) * 256].rearrange("p (h s) -> p h s", h=GQ),
                                                   mid[:, 0, at[0], at[1]], ALU.subtract)
                last.then_inc(tr_free, 1)

            def add_res(g, p, scale):
                s = p % 2
                dve.wait_ge(o_free, NP * g + p + 2)
                dve.wait_ge(res_in[s], 16 * (2 * g + p // 2 + 1))
                nc.vector.scalar_tensor_tensor(out=xres[:, s, :], in0=Q[s][:], scalar=scale, in1=xres[:, s, :],
                                               op0=ALU.mult, op1=ALU.add).then_inc(q_free[s], 1)

            def body_a(g, nxt):
                at = 2 * SA_ * g
                for h in range(GQ):
                    q_max(g, h)
                    if h:
                        q_low(g, h - 1)
                for j in range(1, KVH):
                    for i in range(NP):
                        q_max(g, GQ * j + i)
                        q_low(g, GQ * j + i - 1)
                        n = NP * (j - 1) + i
                        normalise(g, n, at)
                        if n >= 1:
                            mid_low(g, n - 1)
                q_low(g, H - 1)
                for i in range(NP):
                    cond_low(g + 1, i)
                    mid_low(g, NP * (KVH - 1) + i - 1)
                    normalise(g, NP * (KVH - 1) + i, at)
                mid_low(g, NP * KVH - 1)
                if nxt == 0:
                    for p in range(NP):
                        k_bias(g + 1, p)
                        v_bias(g + 1, p)
                        k_max(g + 1, p)
                        add_res(g, p, 1.0 / (WS * AS))
                        kvprod_low(g + 1, p)
                else:
                    late_low(0, 8)
                    route(g + 1, 2 * SA_ * NG)
                    for p in range(NP):
                        add_res(g, p, 1.0 / (WS * AS))
                        late_low(8 + 6 * p, 14 + 6 * p)

            def late_low(c0, c1):
                for c in range(c0, c1):
                    dve.wait_ge(st_hi, c + 1)
                    nc.vector.scalar_tensor_tensor(out=late_chunk_at(c, 1), in0=stages[c % 4], scalar=WS,
                                                   in1=late_chunk_at(c, 0), op0=ALU.mult, op1=ALU.subtract).then_inc(st_lo, 1)

            R_OWN = 3 + 2 * NP + 2

            def route(g, at):
                dve.wait_ge(routed, g - NG + 1)
                nc.vector.scalar_tensor_tensor(out=lg[:], in0=M[:, 0, 0:NP * NB].rearrange("p (a n) -> p a n", a=NP),
                                               scalar=1.0, in1=brb[:].unsqueeze(1).to_broadcast([128, NP, NB]),
                                               op0=ALU.mult, op1=ALU.add).then_inc(lg_read, 1)
                dve.wait_ge(lg_read, g - NG + 1)
                nc.vector.tensor_reduce(mx[:], lg[:], AX.X, ALU.max).then_inc(dve_own, 1)
                dve.wait_ge(dve_own, at + 1)
                nc.vector.tensor_tensor(lg[:], lg[:], mx[:].unsqueeze(2).to_broadcast([128, NP, NB]), ALU.subtract)\
                    .then_inc(dve_own, 1)
                dve.wait_ge(dve_own, at + 2)
                nc.vector.tensor_scalar(lg[:], lg[:], UNDERFLOW, None, ALU.max).then_inc(dve_own, 1)
                dve.wait_ge(dve_own, at + 3)
                nc.vector.memset(pad[:], 0.0)
                for p in range(NP):
                    nc.vector.max(top[:, p, :], lg[:, p, :]).then_inc(dve_own, 1)
                dve.wait_ge(dve_own, at + 3 + NP)
                nc.vector.memset(pad[:], 0.0)
                for p in range(NP):
                    nc.vector.max_index(topi[:, p, :], top[:, p, :], lg[:, p, :]).then_inc(dve_own, 1)
                dve.wait_ge(dve_own, at + 3 + 2 * NP)
                nc.vector.tensor_copy(topf[:], topi[:]).then_inc(dve_own, 1)
                dve.wait_ge(dve_own, at + 4 + 2 * NP)
                for p in range(NP):
                    last = nc.vector.tensor_tensor(eq[:, p, :, :], topf[:, p, 0:TOPK].unsqueeze(2).to_broadcast([128, TOPK, NB]),
                                                   iota[:].unsqueeze(1).to_broadcast([128, TOPK, NB]), ALU.is_equal)
                last.then_inc(dve_own, 1)
                dve.wait_ge(dve_own, at + 5 + 2 * NP)
                nc.vector.tensor_reduce(mask[:], eq.rearrange("p a k n -> p a n k"), AX.X, ALU.add).then_inc(masked, 1)

            def gelu_mask(g, h):
                s = h % 2
                dve.wait_ge(q_free[s], (SQ_ // 2) * g + h // 2 + 2)
                dve.wait_ge(spread, NB * (g - NG) + h + 1)
                nc.vector.tensor_tensor(e[:, s, :], e[:, s, :], TR[s][:], ALU.mult).then_inc(e_ready, 1)

            def gelu_low(g, h):
                dve.wait_ge(e_hi, H * g + h + 1)
                nc.vector.tensor_tensor(mid[:, 1, h, :], e[:, h % 2, :], mid[:, 0, h, :], ALU.subtract).then_inc(e_free, 1)

            def body_b(g, more):
                for h in range(H):
                    gelu_mask(g, h)
                    if h:
                        gelu_low(g, h - 1)
                gelu_low(g, H - 1)
                if more:
                    for p in range(NP):
                        cond_low(g + 1, p)
                for p in range(NP):
                    add_res(g, p, 1.0 / WS)
                    if more and p == 0:
                        route(g + 1, 2 * SA_ * NG + R_OWN * (g + 1 - NG))

            def weight_low(c0, c1):
                for c in range(c0, c1):
                    dve.wait_ge(w_hi, c + 1)
                    nc.vector.scalar_tensor_tensor(out=chunk_at(c, 1), in0=wstage[:, c % 16, :], scalar=WS,
                                                   in1=chunk_at(c, 0), op0=ALU.mult, op1=ALU.subtract).then_inc(w_lo, 1)

            weight_low(0, 4)
            cond_low(0, 0)
            cond_low(0, 1)
            weight_low(4, 8)
            cond_low(0, 2)
            cond_low(0, 3)
            for p in range(NP):
                k_bias(0, p)
                v_bias(0, p)
                k_max(0, p)
                kvprod_low(0, p)
                weight_low(8 + 4 * p, 12 + 4 * p)
            weight_low(24, 40)
            with dve.Fori(0, NG - 1) as g:
                body_a(g, 0)
            body_a(NG - 1, 1)
            with dve.Fori(NG, 2 * NG - 1) as g:
                body_b(g, True)
            body_b(2 * NG - 1, False)

        @block.tensor
        def _(pe):
            pe.sem_inc(heads_free, A_CR)
            pe.sem_inc(t_free, 2)
            pe.sem_inc(o_free, 1)
            pe.wait_ge(pool_consts, 6)
            pe.wait_ge(dve_consts, 5)

            def product(out, lhs, rhs, k, n):
                for q, (a, b) in enumerate(PASSES):
                    last = nc.tensor.matmul(out, lhs(a), rhs(b), start=(k == 0 and q == 0),
                                            stop=(k == n - 1 and q == len(PASSES) - 1))
                return last

            def cond(g, p, f):
                s = p % 2
                pe.wait_ge(x_lo, g * NP + p + 1)
                if not (isinstance(g, int) and g == 0 and p < 2):
                    pe.wait_ge(f_read, f + p - 1)
                for k in range(KC):
                    last = product(F[s][:, k * 128:(k + 1) * 128], lambda a: xs[:, s, a, k * 128:(k + 1) * 128],
                                   lambda b: cws[:, s, b, :], 0, 1)
                last.then_inc(cond_done, 1)

            def kv_project(g, p, f):
                for n, (w, done) in enumerate(((wk, k_done), (wv, v_done))):
                    pe.wait_ge(f_read, f + (4 + 6 * p + n - 1 if p or n else NP))
                    for k in range(KC):
                        last = product(F[n][:], lambda a: hT[:, a, k, p * 128:(p + 1) * 128], lambda b: w[:, b, k, :], k, KC)
                    last.then_inc(done, 1)

            def kv_product(g, p, f):
                s = p % 2
                pe.wait_ge(sk_lo, g * NP + p + 1)
                pe.wait_ge(vs_lo, g * NP + p + 1)
                for n in range(4):
                    jj, b = n // 2, n % 2
                    pe.wait_ge(f_read, f + 6 + 6 * p + n - 1)
                    rows = slice(64 * b, 64 * b + 64)
                    for t in range(2):
                        j = 2 * jj + t
                        last = product(F[b][:, t * DV:(t + 1) * DV], lambda a: sk[rows, s, a, j * D:(j + 1) * D],
                                       lambda c: vs[rows, s, c, j, :], 0, 1)
                    last.then_inc(kv_done, 1)

            def wide(g, h):
                pe.wait_ge(q_free[h % 2], (SQ_ // 2) * g + h // 2 + 1)
                for k in range(KC):
                    last = product(Q[h % 2][:], lambda a: wa[:, a, k, h * D:(h + 1) * D], lambda b: hT[:, b, k, :], k, KC)
                last.then_inc(q_done, 1)

            def heads(g, n):
                j, i = n // NP, n % NP
                pe.wait_ge(e_free, H * g + GQ * j + GQ - 1 + 3)
                pe.wait_ge(m_free, SA_ * g + n + 1)
                for b in range(2):
                    for t in range(2):
                        last = product(M[:, b, t * DV:(t + 1) * DV],
                                       lambda a: sq[:, j % 2, a, 2 * i + b, 2 * t:2 * t + 2, :].rearrange("p h s -> p (h s)"),
                                       lambda c: kv[:, c, 2 * i + b, j, :], 0, 1)
                last.then_inc(heads_free, 1)

            def turn(g, n):
                pe.wait_ge(m_free, SA_ * g + n + 2)
                pe.wait_ge(tr_free, SA_ * g + n + 1)
                for t in range(4):
                    last = nc.tensor.transpose(TR[n % 2][:, t * 128:(t + 1) * 128], att[:, n % 2, t, :], ident[:])
                last.then_inc(t_free, 1)

            def output(g, p, w2=False):
                pe.wait_ge(q_free[p % 2], (SQ_ // 2) * g + H // 2 + p // 2 + 1)
                for h in range(H):
                    last = product(Q[p % 2][:], lambda a: mid[:, a, h, p * 128:(p + 1) * 128], lambda b: (w2s[b] if w2 else wb[:, b])[:, h, :], h, H)
                last.then_inc(o_free, 1)

            def router(g):
                if not (isinstance(g, int) and g == NG):
                    pe.wait_ge(lg_read, g - NG)
                else:
                    pe.wait_ge(m_free, SA_ * NG + 1)
                for p in range(NP):
                    for k in range(KC):
                        last = product(M[:, 0, p * NB:(p + 1) * NB], lambda a: hT[:, a, k, p * 128:(p + 1) * 128],
                                       lambda b: wr[:, b, k, :], k, KC)
                last.then_inc(routed, 1)

            def turn_mask(g):
                pe.wait_ge(masked, g - NG + 1)
                if not (isinstance(g, int) and g == NG):
                    pe.wait_ge(maskT_sb, g - NG)
                for p in range(NP):
                    last = nc.tensor.transpose(M[0:NB, 1, p * 128:(p + 1) * 128], mask[:, p, :], ident[:])
                last.then_inc(maskT_ps, 1)

            def spread_mask(g, h):
                if h == 0:
                    pe.wait_ge(maskT_sb, g - NG + 1)
                    pe.wait_ge(tr_free, SA_ * NG + 2)
                pe.wait_ge(e_ready, H * g + h - 1)
                nc.tensor.matmul(TR[h % 2][:], sel[:, h, :], maskT[:], start=True, stop=True).then_inc(spread, 1)

            def body_a(g, nxt, f):
                for h in range(GQ):
                    wide(g, h)
                for j in range(1, KVH):
                    for i in range(NP):
                        wide(g, GQ * j + i)
                        n = NP * (j - 1) + i
                        if j == 1 and i == 0:
                            pe.wait_ge(f_read, f)
                        heads(g, n)
                        if n >= 1:
                            turn(g, n - 1)
                for i in range(NP):
                    cond(g + 1, i, f)
                    turn(g, NP * (KVH - 1) + i - 1)
                    heads(g, NP * (KVH - 1) + i)
                if nxt == 0:
                    kv_project(g + 1, 0, f)
                    turn(g, NP * KVH - 1)
                    for p in range(NP):
                        if p:
                            kv_project(g + 1, p, f)
                        if p == 0:
                            pe.wait_ge(tr_free, SA_ * g + SA_ + 2)
                        output(g, p)
                        kv_product(g + 1, p, f)
                else:
                    pe.wait_ge(f_read, f + NP)
                    router(g + 1)
                    turn(g, NP * KVH - 1)
                    pe.wait_ge(tr_free, SA_ * g + SA_ + 2)
                    for p in range(NP):
                        output(g, p)
                        if p == 1:
                            turn_mask(g + 1)

            def body_b(g, more, f):
                for h in range(H):
                    wide(g, h)
                    spread_mask(g, h)
                if more:
                    for p in range(NP):
                        cond(g + 1, p, f)
                    pe.wait_ge(f_read, f + NP)
                    router(g + 1)
                pe.wait_ge(e_free, H * g + H - 1 + 3)
                for p in range(NP):
                    output(g, p, w2=True)
                    if more and p == 1:
                        turn_mask(g + 1)

            for p in range(NP):
                cond(0, p, 0)
            pe.wait_ge(w_lo, 8)
            for p in range(NP):
                kv_project(0, p, 0)
                kv_product(0, p, 0)
            pe.wait_ge(w_lo, 40)
            with pe.Fori(0, NG - 1) as g:
                body_a(g, 0, (g + 1) * SF_)
            body_a(NG - 1, 1, front_use(NG, 0))
            pe.wait_ge(st_lo, 32)
            with pe.Fori(NG, 2 * NG - 1) as g:
                body_b(g, True, SF_ * NG + NP * (g + 1 - NG))
            body_b(2 * NG - 1, False, None)


_SHAPE = (B, C, T)


def kernel(**inputs):
    import numpy as _np
    import concourse.bacc as _bacc
    from concourse import mybir as _mybir
    from concourse.bass_utils import run_bass_kernel_spmd as _run

    nc = _bacc.Bacc("TRN2", target_bir_lowering=False, num_devices=1)
    arr = {k: _np.asarray(v) for k, v in inputs.items()}
    laid = {
        "x": arr["x"], "i1": arr["itok_B_0_7"], "i2": arr["itok_B_1_198"],
        "cw": arr["L0_cond_weights"], "cw2": arr["L0_cond2_weights"],
        "wq": arr["L0_attn_Wq"].T, "wk": arr["L0_attn_Wk"].T, "wv": arr["L0_attn_Wv"].T, "wo": arr["L0_attn_Wo"].T,
        "bq": arr["L0_attn_bq"].reshape(H, D).T, "bk": arr["L0_attn_bk"], "bv": arr["L0_attn_bv"],
        "wr": arr["L0_ffn_Wr"].T, "br": arr["L0_ffn_br"], "w1": arr["L0_ffn_W1"].T, "w2": arr["L0_ffn_W2"].T,
    }
    arrays, args = {}, []
    for name, a in laid.items():
        a = _np.ascontiguousarray(a)
        arrays[f"in_{name}_dram"] = a
        args.append(nc.dram_tensor(f"in_{name}_dram", a.shape, _mybir.dt.from_np(a.dtype), kind="ExternalInput").ap())
    args.append(nc.dram_tensor("x1_dram", _SHAPE, _mybir.dt.float32, kind="Internal").ap())
    args.append(nc.dram_tensor("out_0_dram", _SHAPE, _mybir.dt.float32, kind="ExternalOutput").ap())
    adaln_attn_ffn(nc, *args)
    r = _run(nc, [arrays], core_ids=[0])
    return r.results[0]["out_0_dram"]
```

```python
import concourse.bass as bass
from concourse import mybir
from contextlib import ExitStack

F32 = mybir.dt.float32
F16 = mybir.dt.float16
I32 = mybir.dt.int32
U32 = mybir.dt.uint32
ALU = mybir.AluOpType
ACT = mybir.ActivationFunctionType
AX = mybir.AxisListType

B, C, T = 32, 64, 512
H, KVH, D = 16, 4, 128
GQ = H // KVH
NB, TOPK = 16, 4
KC = T // 128
GB = 8
NG = B // GB
TOK = GB * C
NP = GB // 2
DV = D + 1
WS = 32.0
AS = 16.0
EPS = 1e-6
UNDERFLOW = -104.0
SP_, SQ_, SA_, SF_ = NP, H + NP, KVH * NP, NP + 6 * NP
A_CR = 8


def adaln_attn_ffn(nc, x_d, i1_d, i2_d, cw_d, cw2_d, wq_d, wk_d, wv_d, wo_d, bq_d, bk_d, bv_d,
                   wr_d, br_d, w1_d, w2_d, x1_d, mask_d, out_d):
    ctx = ExitStack()
    with ctx:
        def sb(name, shape, dt):
            return ctx.enter_context(nc.sbuf_tensor(name, shape, dt))

        def pb(name):
            return ctx.enter_context(nc.psum_tensor(name, [128, 512], F32))

        def sem(name):
            return ctx.enter_context(nc.semaphore(name))

        wa = sb("wa", [128, 2, KC, H * D], F16)
        wb = sb("wb", [128, 2, H, T], F16)
        wk = sb("wk", [128, 2, KC, KVH * D], F16)
        wv = sb("wv", [128, 2, KC, KVH * D], F16)
        wr = sb("wr", [128, 2, KC, NB], F16)
        wr32 = sb("wr32", [128, KC, NB], F32)
        bq = sb("bq", [128, H], F32)
        bq1 = sb("bq1", [128, H], F32)
        bk1 = sb("bk1", [128, KVH * D], F32)
        bv = sb("bv", [128, KVH * D], F32)
        brb = sb("brb", [128, NB], F32)
        negone = sb("negone", [128, 1], F32)
        zero = sb("zero", [128, 1], F32)
        idx = sb("idx", [1, 2, B], I32)
        ident = sb("ident", [128, 128], F32)
        iota = sb("iota", [128, NB], F32)
        stage = sb("stage", [128, 2, 512], F32)
        xin = sb("xin", [128, 2, T], F32)
        xs = sb("xs", [128, 2, 2, T], F16)
        cw = sb("cw", [128, 2, 128], F32)
        cws = sb("cws", [128, 2, 2, 128], F16)
        hT = sb("hT", [128, 2, KC, TOK], F16)
        ku = sb("ku", [128, KVH * D], F32)
        kvf = sb("kvf", [128, 2, KVH * D], F32)
        kf, vf = kvf[:, 0, :], kvf[:, 1, :]
        sk = sb("sk", [128, 2, 2, KVH * D], F16)
        vs = sb("vs", [128, 2, 2, KVH, DV], F16)
        kv = sb("kv", [128, 2, GB, KVH, DV], F16)
        e = sb("e", [128, 2, TOK], F32)
        u = sb("u", [128, 2, TOK], F32)
        sq = sb("sq", [128, 2, 2, GB, GQ, C], F16)
        att = sb("att", [128, 2, 4, 128], F32)
        den = sb("den", [128, 4], F32)
        rden = sb("rden", [128, 4], F32)
        mid = sb("mid", [128, 2, H, TOK], F16)
        xres = sb("xres", [128, 2, T], F32)
        w2s = (kv[:].rearrange("p a b j d -> p (a b j d)")[:, 0:H * T].rearrange("p (h t) -> p h t", h=H),
               sq[:].rearrange("p s a b h c -> p (s a b h c)").rearrange("p (h t) -> p h t", h=H))
        stages = (stage, kvf, e, u)
        wstage = mid[:].rearrange("p a h t -> p (a h t)").bitcast(F32).rearrange("p (c n) -> p c n", n=512)
        lg = sb("lg", [128, NP, NB], F32)
        mx = sb("mx", [128, NP], F32)
        top = sb("top", [128, NP, 8], F32)
        topi = sb("topi", [128, NP, 8], U32)
        topf = sb("topf", [128, NP, 8], F32)
        eq = ku[:, 0:NP * TOPK * NB].rearrange("p (a k n) -> p a k n", a=NP, k=TOPK)
        mask = sb("mask", [128, NP, NB], F32)
        pad = sb("pad", [128, 1], F32)
        maskT = sb("maskT", [NB, TOK], F16)
        maskb = tuple(w[:].rearrange("p a k n -> p (a k) n") for w in (wk, wv))

        Q = [pb(f"Q{i}") for i in range(2)]
        F = [pb(f"F{i}") for i in range(2)]
        M = ctx.enter_context(nc.psum_tensor("M", [128, 2, 512], F32))
        TR = [pb(f"TR{i}") for i in range(2)]

        idx_in = [sem(f"idx_in{i}") for i in range(2)]
        bias_in = sem("bias_in")
        consts_in = sem("consts_in")
        pool_consts = sem("pool_consts")
        dve_consts = sem("dve_consts")
        act_consts = sem("act_consts")
        w_in = [sem(f"w_in{i}") for i in range(4)]
        w_hi = sem("w_hi")
        w_lo = sem("w_lo")
        st_in = [sem(f"st_in{i}") for i in range(4)]
        st_hi = sem("st_hi")
        st_lo = sem("st_lo")
        x_in = [sem(f"x_in{i}") for i in range(2)]
        x_hi = sem("x_hi")
        x_lo = sem("x_lo")
        cond_done = sem("cond_done")
        hT_hi = sem("hT_hi")
        f_read = sem("f_read")
        k_done = sem("k_done")
        v_done = sem("v_done")
        k_exp = sem("k_exp")
        k_elu = sem("k_elu")
        sk_hi = sem("sk_hi")
        sk_lo = sem("sk_lo")
        vs_hi = sem("vs_hi")
        vs_lo = sem("vs_lo")
        kv_done = sem("kv_done")
        kv_hi = sem("kv_hi")
        q_done = sem("q_done")
        q_free = [sem(f"q_free{i}") for i in range(2)]
        e_ready = sem("e_ready")
        e_hi = sem("e_hi")
        e_free = sem("e_free")
        heads_free = sem("heads_free")
        m_free = sem("m_free")
        t_free = sem("t_free")
        mid_hi = sem("mid_hi")
        tr_free = sem("tr_free")
        o_free = sem("o_free")
        res_in = [sem(f"res_in{i}") for i in range(2)]
        stored = [sem(f"stored{i}") for i in range(2)]
        routed = sem("routed")
        lg_read = sem("lg_read")
        dve_own = sem("dve_own")
        masked = sem("masked")
        maskT_ps = sem("maskT_ps")
        maskT_sb = sem("maskT_sb")
        mask_out = sem("mask_out")
        mask_in = [sem(f"mask_in{i}") for i in range(4)]

        CONDS = [("cond", p, 0) for p in range(NP)]
        KVS = [("kv", p, n) for p in range(NP) for n in range(4)]
        PROJ = [(w, p, 0) for p in range(NP) for w in ("k", "v")]
        STEADY = CONDS + PROJ[:4] + KVS[:4] + PROJ[4:6] + KVS[4:8] + PROJ[6:8] + KVS[8:]
        FIRST = CONDS[:2] + PROJ[:2] + CONDS[2:] + STEADY[6:]

        def bank(order, use):
            kind, p, n = use
            if kind == "kv" and order is FIRST:
                return (M[:, 0, :], M[:, 1, :], TR[0], TR[1])[n], 2 + n
            i = {"cond": p % 2, "k": 0, "v": 1, "kv": n % 2}[kind]
            return F[i], i

        def read(order, kind, p, n=0):
            return order.index((kind, p, n)) + 1

        def bank_read(order, kind, p, n=0):
            at = order.index((kind, p, n))
            same = [i for i in range(at) if bank(order, order[i])[1] == bank(order, order[at])[1]]
            return same[-1] + 1 if same else None

        UNITS = [(w, k, 0) for w in range(2) for k in range(0, KC, 2)]
        UNITS += [(2, k, j) for j in range(KVH) for k in range(0, KC, 2)] + [(3, h, 0) for h in range(0, H, 2)]
        W_Q, W_O, W_ALL = 4, 12, 20
        S_1, S_ALL = 8, 16

        def unit_at(v, part):
            w, rows, cols = UNITS[v]
            if w == 3:
                return wb[:, part, rows:rows + 2, :]
            return (wk, wv, wa)[w][:, part, rows:rows + 2, cols * 512:(cols + 1) * 512]

        def late_unit_at(v, part):
            if v < S_1:
                return wa[:, part, 2 * (v % 2):2 * (v % 2) + 2, v // 2 * 512:(v // 2 + 1) * 512]
            return w2s[part][:, 2 * (v - S_1):2 * (v - S_1) + 2, :]

        PASSES = ((0, 0), (0, 1), (1, 0))

        block = ctx.enter_context(nc.Block())

        @block.sync
        def _(sp):
            for q in stored:
                sp.sem_inc(q, 16)
            sp.dma_start(idx[0:1, 0, :], i1_d.rearrange("(a n) -> a n", a=1)).then_inc(idx_in[0], 16)

            def load_x(g, p, layer):
                s = p % 2
                src, w_d, n = (x_d, cw_d, 8) if layer == 0 else (x1_d, cw2_d, 200)
                t = (g - NG * layer) * GB + 2 * p
                if not (isinstance(g, int) and g == 0 and p < 2):
                    sp.wait_ge(x_lo, g * NP + p - 1)
                if layer == 1:
                    sp.wait_ge(stored[s], 16 * (2 * (g - NG) + p // 2 + 2))
                sp.dma_start(xin[:, s, :], src[bass.ds(t, 2), :, :].rearrange("b c t -> (b c) t")).then_inc(x_in[s], 16)
                if isinstance(g, int) and g == 0 and p == 0:
                    sp.wait_ge(idx_in[0], 16)
                    sp.wait_ge(pool_consts, 1)
                for h in range(2):
                    i = sp.value_load(idx[0:1, layer, bass.ds(t + h, 1)], min_val=0, max_val=n - 1)
                    sp.dma_start(cw[64 * h:64 * h + 64, s, 64 * h:64 * h + 64],
                                 w_d[bass.ds(i, 1), :, :].rearrange("a c d -> (a c) d")).then_inc(x_in[s], 16)

            def load_res(g, p, layer):
                s = p % 2
                t = (g - NG * layer) * GB + 2 * p
                sp.wait_ge(stored[s], 16 * (2 * g + p // 2 + 1))
                sp.dma_start(xres[:, s, :], (x1_d if layer else x_d)[bass.ds(t, 2), :, :]
                             .rearrange("b c t -> (b c) t")).then_inc(res_in[s], 16)

            def store(g, p, layer):
                s = p % 2
                t = (g - NG * layer) * GB + 2 * p
                sp.wait_ge(q_free[s], (SQ_ // 2) * g + H // 2 + p // 2 + 2)
                sp.dma_start((out_d if layer else x1_d)[bass.ds(t, 2), :, :]
                             .rearrange("b c t -> (b c) t"), xres[:, s, :]).then_inc(stored[s], 16)

            def body(g, layer, nxt):
                if nxt is not None:
                    load_x(g + 1, 0, nxt)
                    load_x(g + 1, 1, nxt)
                load_res(g, 0, layer)
                load_res(g, 1, layer)
                if nxt is not None:
                    load_x(g + 1, 2, nxt)
                    load_x(g + 1, 3, nxt)
                store(g, 0, layer)
                load_res(g, 2, layer)
                store(g, 1, layer)
                load_res(g, 3, layer)
                store(g, 2, layer)
                store(g, 3, layer)

            def load_weights(q):
                w, rows, cols = UNITS[2 * q]
                w_d = (wk_d, wv_d, wq_d, wo_d)[w]
                if q >= 4:
                    sp.wait_ge(w_lo, 2 * (q - 3))
                sp.dma_start(wstage[:, 4 * (q % 4):4 * (q % 4) + 4, :],
                             w_d[rows * 128:(rows + 4) * 128, cols * 512:(cols + 1) * 512]
                             .rearrange("(k p) n -> p k n", p=128)).then_inc(w_in[q % 4], 16)

            load_x(0, 0, 0)
            load_x(0, 1, 0)
            load_weights(1)
            for n, (b_sb, b_d) in enumerate(((bk1, bk_d), (bv, bv_d))):
                sp.dma_start(b_sb[:], b_d.rearrange("(a n) -> a n", a=1).to_broadcast([128, 512])).then_inc(bias_in, 16)
                load_x(0, 2 + n, 0)
            sp.dma_start(bq[:], bq_d).then_inc(consts_in, 16)
            sp.dma_start(brb[:], br_d.rearrange("(a n) -> a n", a=1).to_broadcast([128, NB])).then_inc(consts_in, 16)
            sp.dma_start(wr32[:], wr_d.rearrange("(k p) n -> p k n", p=128)).then_inc(consts_in, 16)
            for q in range(2, 10):
                load_weights(q)
            sp.dma_start(idx[0:1, 1, :], i2_d.rearrange("(a n) -> a n", a=1)).then_inc(idx_in[1], 16)
            sp.wait_ge(idx_in[1], 16)
            with sp.Fori(0, NG - 1) as g:
                body(g, 0, 0)
            body(NG - 1, 0, 1)
            with sp.Fori(NG, 2 * NG - 1) as g:
                body(g, 1, 1)
            body(2 * NG - 1, 1, None)
            for q in stored:
                sp.wait_ge(q, 16 * (4 * NG + 1))

        @block.gpsimd
        def _(pool):
            pool.memset(cw[:], 0.0).then_inc(pool_consts, 1)
            pool.memset(ident[:], 0.0).then_inc(pool_consts, 1)
            pool.iota(iota[:], pattern=[[1, NB]], base=0, channel_multiplier=0,
                      allow_small_or_imprecise_dtypes=True).then_inc(pool_consts, 1)
            pool.wait_ge(pool_consts, 3)
            pool.affine_select(out=ident[:], in_=ident[:], compare_op=ALU.not_equal, fill=1.0, base=0,
                               pattern=[[-1, 128]], channel_multiplier=1).then_inc(pool_consts, 1)

            def x_split(g, p):
                s = p % 2
                pool.wait_ge(x_hi, g * NP + p + 1)
                pool.tensor_tensor(xs[:, s, 1, :], xin[:, s, :], xs[:, s, 0, :], ALU.subtract)
                pool.tensor_tensor(cws[:, s, 1, :], cw[:, s, :], cws[:, s, 0, :], ALU.subtract).then_inc(x_lo, 1)

            def kv_split(g, p):
                s = p % 2
                pool.wait_ge(sk_hi, g * NP + p + 1)
                pool.tensor_tensor(sk[:, s, 1, :], kf, sk[:, s, 0, :], ALU.subtract).then_inc(sk_lo, 1)
                pool.wait_ge(vs_hi, g * NP + p + 1)
                pool.tensor_tensor(vs[:, s, 1, :, 0:D], vf.rearrange("p (h d) -> p h d", h=KVH),
                                   vs[:, s, 0, :, 0:D], ALU.subtract).then_inc(vs_lo, 1)

            x_split(0, 0)
            x_split(0, 1)
            x_split(0, 2)
            x_split(0, 3)
            for p in range(NP):
                kv_split(0, p)
            with pool.Fori(0, NG - 1) as g:
                for p in range(NP):
                    x_split(g + 1, p)
                for p in range(NP):
                    kv_split(g + 1, p)
            for p in range(NP):
                x_split(NG, p)
            with pool.Fori(NG, 2 * NG - 1) as g:
                for p in range(NP):
                    x_split(g + 1, p)

        @block.scalar
        def _(act):
            act.dma_start(wstage[:, 0:4, :], wk_d.rearrange("(k p) n -> p k n", p=128)).then_inc(w_in[0], 16)

            def constants():
                act.wait_ge(consts_in, 48)
                act.wait_ge(dve_consts, 3)
                nc.scalar.activation(bq1[:], bq[:], ACT.Identity, bias=1.0).then_inc(act_consts, 1)
                nc.scalar.activation(wr[:, 0, :, :], wr32[:], ACT.Copy).then_inc(act_consts, 1)

            def x_high(g, p):
                s = p % 2
                act.wait_ge(x_in[s], 48 * (2 * g + p // 2 + 1))
                if not (isinstance(g, int) and g == 0 and p < 2):
                    act.wait_ge(cond_done, g * NP + p - 1)
                nc.scalar.activation(xs[:, s, 0, :], xin[:, s, :], ACT.Copy)
                nc.scalar.activation(cws[:, s, 0, :], cw[:, s, :], ACT.Copy).then_inc(x_hi, 1)

            def cond_high(g, p):
                act.wait_ge(cond_done, g * NP + p + 1)
                if not (isinstance(g, int) and g == 0):
                    act.wait_ge(q_done, H * g)
                nc.scalar.activation(hT[:, 0, :, p * 128:(p + 1) * 128], F[p % 2][:].rearrange("p (k n) -> p k n", k=KC),
                                     ACT.Copy).then_inc(hT_hi, 1)

            def k_expo(g, p, f, order=STEADY):
                act.wait_ge(f_read, f + read(order, "k", p))
                if not (isinstance(g, int) and g == 0 and p == 0):
                    act.wait_ge(sk_lo, g * NP + p)
                nc.scalar.activation(kf, ku[:], ACT.Exp, bias=negone[:]).then_inc(k_exp, 1)

            def k_high(g, p):
                s = p % 2
                act.wait_ge(k_elu, g * NP + p + 1)
                if not (isinstance(g, int) and g == 0 and p < 2):
                    act.wait_ge(kv_done, 4 * (g * NP + p - 1))
                nc.scalar.activation(sk[:, s, 0, :], kf, ACT.Copy).then_inc(sk_hi, 1)

            def v_high(g, p, f, order=STEADY):
                s = p % 2
                act.wait_ge(f_read, f + read(order, "v", p))
                nc.scalar.activation(vs[:, s, 0, :, 0:D], vf.rearrange("p (h d) -> p h d", h=KVH),
                                     ACT.Copy).then_inc(vs_hi, 1)

            def kvprod_high(g, p, order=STEADY):
                for n in range(4):
                    jj, b = n // 2, n % 2
                    act.wait_ge(kv_done, 4 * (g * NP + p) + n + 1)
                    act.wait_ge(heads_free, SA_ * g + A_CR)
                    nc.scalar.activation(kv[:, 0, 2 * p + b, 2 * jj:2 * jj + 2, :],
                                         bank(order, ("kv", p, n))[0][:, 0:2 * DV].rearrange("p (j d) -> p j d", j=2), ACT.Copy).then_inc(kv_hi, 1)

            def q_read(g, h):
                s = h % 2
                act.wait_ge(q_done, H * g + h + 1)
                act.wait_ge(e_free, H * g + h + 1)
                nc.scalar.activation(e[:, s, :], Q[s][:], ACT.Exp, bias=bq[:, h:h + 1], scale=1.0 / WS)
                nc.scalar.activation(u[:, s, :], Q[s][:], ACT.Identity, bias=bq1[:, h:h + 1],
                                     scale=1.0 / WS).then_inc(q_free[s], 1)

            def q_high(g, h):
                act.wait_ge(e_ready, H * g + h + 1)
                act.wait_ge(heads_free, SA_ * g + 4 * (h // GQ) - 4 + A_CR)
                nc.scalar.activation(sq[:, (h // GQ) % 2, 0, :, h % GQ, :],
                                     e[:, h % 2, :].rearrange("p (b s) -> p b s", b=GB), ACT.Copy).then_inc(e_hi, 1)

            def mid_high(g, n):
                j, i = n // NP, n % NP
                act.wait_ge(t_free, SA_ * g + n + 3)
                act.wait_ge(o_free, NP * g + 1)
                for b in range(2):
                    last = nc.scalar.activation(
                        mid[:, 0, GQ * j:GQ * j + GQ, (2 * i + b) * C:(2 * i + b + 1) * C],
                        TR[n % 2][:, b * 256:(b + 1) * 256].rearrange("p (h s) -> p h s", h=GQ), ACT.Copy)
                last.then_inc(mid_hi, 1)

            def fetch(v):
                if v >= S_ALL:
                    return
                if v >= 4:
                    act.wait_ge(st_lo, v - 3)
                elif v == 1:
                    act.wait_ge(sk_lo, NP * NG)
                    act.wait_ge(vs_lo, NP * NG)
                elif v >= 2:
                    act.wait_ge(e_free, H * NG + 2)
                w_d, rows, cols = (w1_d, 2 * (v % 2), v // 2) if v < S_1 else (w2_d, 2 * (v - S_1), 0)
                act.dma_start(stages[v % 4][:], w_d[rows * 128:(rows + 2) * 128, cols * 512:(cols + 1) * 512]
                              .rearrange("(k p) n -> p k n", p=128)).then_inc(st_in[v % 4], 16)

            def late_high(v0, v1):
                for v in range(v0, v1):
                    if v:
                        fetch(v + 3)
                    act.wait_ge(st_in[v % 4], 16 * (v // 4 + 1))
                    if v == 0:
                        act.wait_ge(q_done, H * NG)
                    if v == S_1:
                        act.wait_ge(heads_free, SA_ * NG + A_CR)
                    nc.scalar.activation(late_unit_at(v, 0), stages[v % 4][:], ACT.Copy, scale=WS).then_inc(st_hi, 1)

            def body_a(g, nxt, f):
                if nxt == 1:
                    fetch(0)
                    fetch(1)
                for h in range(H):
                    q_read(g, h)
                    if h:
                        q_high(g, h - 1)
                    if h >= 7:
                        mid_high(g, h - 7)
                    if h in (8, 9):
                        x_high(g + 1, h - 8)
                    if h == 14:
                        x_high(g + 1, 2)
                    if h == 15:
                        x_high(g + 1, 3)
                q_high(g, H - 1)
                mid_high(g, 9)
                if nxt == 1:
                    fetch(2)
                    fetch(3)
                cond_high(g + 1, 0)
                cond_high(g + 1, 1)
                mid_high(g, 10)
                if nxt == 1:
                    late_high(0, 1)
                cond_high(g + 1, 2)
                mid_high(g, 11)
                if nxt == 1:
                    late_high(1, 2)
                cond_high(g + 1, 3)
                mid_high(g, 12)
                if nxt == 0:
                    k_expo(g + 1, 0, f)
                    mid_high(g, 13)
                    k_high(g + 1, 0)
                    v_high(g + 1, 0, f)
                    mid_high(g, 14)
                    k_expo(g + 1, 1, f)
                    mid_high(g, 15)
                    k_high(g + 1, 1)
                    v_high(g + 1, 1, f)
                    kvprod_high(g + 1, 0)
                    for p in (2, 3):
                        k_expo(g + 1, p, f)
                        k_high(g + 1, p)
                        v_high(g + 1, p, f)
                        kvprod_high(g + 1, p - 1)
                    kvprod_high(g + 1, 3)
                else:
                    late_high(2, 3)
                    mid_high(g, 13)
                    late_high(3, 4)
                    mid_high(g, 14)
                    late_high(4, 6)
                    mid_high(g, 15)
                    late_high(6, 11)
                    mask_high(g + 1)
                    late_high(11, 14)
                    mask_broadcast(g + 1)
                    late_high(14, S_ALL)
                    act.wait_ge(st_lo, S_ALL)

            def mask_high(g):
                act.wait_ge(maskT_ps, g - NG + 1)
                if not (isinstance(g, int) and g == NG):
                    act.wait_ge(mask_out, 16 * (g - NG))
                nc.scalar.activation(maskT[:], M[0:NB, 1, :], ACT.Copy).then_inc(maskT_sb, 1)
                act.wait_ge(maskT_sb, g - NG + 1)
                act.wait_ge(e_ready, H * g)
                act.dma_start(mask_d, maskT[:]).then_inc(mask_out, 16)

            def mask_broadcast(g):
                act.wait_ge(mask_out, 16 * (g - NG + 1))
                for q in range(4):
                    act.dma_start(maskb[q // 2][:, q % 2 * 4:q % 2 * 4 + 4, :].rearrange("p n t -> p (n t)"),
                                  mask_d[4 * q:4 * q + 4, :].rearrange("(a n) t -> a (n t)", a=1)
                                  .to_broadcast([128, 4 * TOK])).then_inc(mask_in[q], 16)

            def gelu_read(g, h):
                s = h % 2
                act.wait_ge(q_done, H * g + h + 1)
                act.wait_ge(e_free, H * g + h + 1)
                nc.scalar.activation(e[:, s, :], Q[s][:], ACT.Gelu, bias=zero[:], scale=1.0 / WS).then_inc(q_free[s], 1)

            def gelu_high(g, h):
                act.wait_ge(e_ready, H * g + h + 1)
                act.wait_ge(o_free, NP * g + 1)
                nc.scalar.activation(mid[:, 0, h, :], e[:, h % 2, :], ACT.Copy).then_inc(e_hi, 1)

            def body_b(g, more):
                for h in range(H):
                    gelu_read(g, h)
                    if h:
                        gelu_high(g, h - 1)
                    if more and h in (8, 9):
                        x_high(g + 1, h - 8)
                    if more and h in (14, 15):
                        x_high(g + 1, h - 12)
                gelu_high(g, H - 1)
                if more:
                    for p in range(NP):
                        cond_high(g + 1, p)
                    mask_high(g + 1)
                    mask_broadcast(g + 1)

            def weight_high(v0, v1):
                for v in range(v0, v1):
                    act.wait_ge(w_in[v // 2 % 4], 16 * (v // 8 + 1))
                    c = 2 * v % 16
                    nc.scalar.activation(unit_at(v, 0), wstage[:, c:c + 2, :], ACT.Copy, scale=WS).then_inc(w_hi, 1)

            weight_high(0, 1)
            x_high(0, 0)
            x_high(0, 1)
            weight_high(1, 2)
            cond_high(0, 0)
            cond_high(0, 1)
            weight_high(2, 4)
            x_high(0, 2)
            x_high(0, 3)
            k_expo(0, 0, 0, FIRST)
            cond_high(0, 2)
            cond_high(0, 3)
            k_high(0, 0)
            v_high(0, 0, 0, FIRST)
            constants()
            for p in range(1, NP):
                v = W_Q + 4 * (p - 1)
                weight_high(v, v + 2)
                k_expo(0, p, 0, FIRST)
                if p < 3:
                    weight_high(v + 2, v + 3)
                k_high(0, p)
                if p < 3:
                    weight_high(v + 3, v + 4)
                v_high(0, p, 0, FIRST)
                kvprod_high(0, p - 1, FIRST)
            weight_high(14, 17)
            kvprod_high(0, 3, FIRST)
            weight_high(17, W_ALL)
            with act.Fori(0, NG - 1) as g:
                body_a(g, 0, (g + 1) * SF_)
            body_a(NG - 1, 1, SF_ * NG)
            with act.Fori(NG, 2 * NG - 1) as g:
                body_b(g, True)
            body_b(2 * NG - 1, False)

        @block.vector
        def _(dve):
            own = [0]

            def step(ins):
                own[0] += 1
                ins.then_inc(dve_own, 1)

            for q in q_free:
                dve.sem_inc(q, 1)
            dve.sem_inc(e_free, 2)
            dve.sem_inc(m_free, 1)
            dve.sem_inc(tr_free, 2)
            nc.vector.memset(negone[:], -1.0).then_inc(dve_consts, 1)
            nc.vector.memset(zero[:], 0.0).then_inc(dve_consts, 1)
            for s in range(2):
                nc.vector.memset(vs[:, s, 0, :, D:DV], 1.0)
                last = nc.vector.memset(vs[:, s, 1, :, D:DV], 0.0)
            last.then_inc(dve_consts, 1)

            def bias_one():
                dve.wait_ge(bias_in, 32)
                nc.vector.tensor_scalar(bk1[:], bk1[:], 1.0, None, ALU.add).then_inc(dve_consts, 1)
                dve.wait_ge(dve_consts, 4)

            def router_low():
                dve.wait_ge(act_consts, 2)
                nc.vector.tensor_tensor(wr[:, 1, :, :], wr32[:], wr[:, 0, :, :], ALU.subtract).then_inc(dve_consts, 1)

            def cond_low(g, p):
                dve.wait_ge(hT_hi, g * NP + p + 1)
                nc.vector.tensor_tensor(hT[:, 1, :, p * 128:(p + 1) * 128], F[p % 2][:].rearrange("p (k n) -> p k n", k=KC),
                                        hT[:, 0, :, p * 128:(p + 1) * 128], ALU.subtract).then_inc(f_read, 1)

            def k_bias(g, p):
                dve.wait_ge(k_done, g * NP + p + 1)
                nc.vector.scalar_tensor_tensor(out=ku[:], in0=F[0][:], scalar=1.0 / WS, in1=bk1[:],
                                               op0=ALU.mult, op1=ALU.add).then_inc(f_read, 1)

            def v_bias(g, p):
                dve.wait_ge(v_done, g * NP + p + 1)
                if not (isinstance(g, int) and g == 0 and p == 0):
                    dve.wait_ge(vs_lo, g * NP + p)
                nc.vector.scalar_tensor_tensor(out=vf, in0=F[1][:], scalar=1.0 / WS, in1=bv[:],
                                               op0=ALU.mult, op1=ALU.add).then_inc(f_read, 1)

            def k_max(g, p):
                dve.wait_ge(k_exp, g * NP + p + 1)
                nc.vector.scalar_tensor_tensor(out=kf, in0=kf, scalar=1.0, in1=ku[:],
                                               op0=ALU.min, op1=ALU.max).then_inc(k_elu, 1)

            def kvprod_low(g, p, order=STEADY):
                for n in range(4):
                    jj, b = n // 2, n % 2
                    dve.wait_ge(kv_hi, 4 * (g * NP + p) + n + 1)
                    nc.vector.tensor_tensor(kv[:, 1, 2 * p + b, 2 * jj:2 * jj + 2, :],
                                            bank(order, ("kv", p, n))[0][:, 0:2 * DV].rearrange("p (j d) -> p j d", j=2),
                                            kv[:, 0, 2 * p + b, 2 * jj:2 * jj + 2, :], ALU.subtract).then_inc(f_read, 1)

            def q_max(g, h):
                s = h % 2
                dve.wait_ge(q_free[s], (SQ_ // 2) * g + h // 2 + 2)
                nc.vector.scalar_tensor_tensor(out=e[:, s, :], in0=e[:, s, :], scalar=1.0, in1=u[:, s, :],
                                               op0=ALU.min, op1=ALU.max).then_inc(e_ready, 1)

            def q_low(g, h):
                dve.wait_ge(e_hi, H * g + h + 1)
                nc.vector.tensor_tensor(sq[:, (h // GQ) % 2, 1, :, h % GQ, :],
                                        e[:, h % 2, :].rearrange("p (b s) -> p b s", b=GB),
                                        sq[:, (h // GQ) % 2, 0, :, h % GQ, :], ALU.subtract).then_inc(e_free, 1)

            def normalise(g, n, at):
                dve.wait_ge(heads_free, SA_ * g + n + 1 + A_CR)
                den_ps = M[:, :, D:2 * DV:DV]
                nc.vector.tensor_scalar(den[:].rearrange("p (a b) -> p a b", a=2), den_ps, EPS, 1.0 / AS,
                                        ALU.add, ALU.mult).then_inc(dve_own, 1)
                dve.wait_ge(dve_own, at + 2 * n + 1)
                nc.vector.reciprocal(rden[:], den[:]).then_inc(dve_own, 1)
                dve.wait_ge(dve_own, at + 2 * n + 2)
                dve.wait_ge(t_free, SA_ * g + n + 1)
                nc.vector.tensor_tensor(att[:, n % 2, :, :].rearrange("p (a b) d -> p a b d", a=2),
                                        M[:, :, 0:2 * DV].rearrange("p a (b d) -> p a b d", b=2)[:, :, :, 0:D],
                                        rden[:].rearrange("p (a b) -> p a b", a=2).unsqueeze(3).to_broadcast([128, 2, 2, D]),
                                        ALU.mult).then_inc(m_free, 1)

            def mid_low(g, n):
                j, i = n // NP, n % NP
                dve.wait_ge(mid_hi, SA_ * g + n + 1)
                for b in range(2):
                    at = (slice(GQ * j, GQ * j + GQ), slice((2 * i + b) * C, (2 * i + b + 1) * C))
                    last = nc.vector.tensor_tensor(mid[:, 1, at[0], at[1]],
                                                   TR[n % 2][:, b * 256:(b + 1) * 256].rearrange("p (h s) -> p h s", h=GQ),
                                                   mid[:, 0, at[0], at[1]], ALU.subtract)
                last.then_inc(tr_free, 1)

            def add_res(g, p, scale):
                s = p % 2
                dve.wait_ge(o_free, NP * g + p + 2)
                dve.wait_ge(res_in[s], 16 * (2 * g + p // 2 + 1))
                nc.vector.scalar_tensor_tensor(out=xres[:, s, :], in0=Q[s][:], scalar=scale, in1=xres[:, s, :],
                                               op0=ALU.mult, op1=ALU.add).then_inc(q_free[s], 1)

            def body_a(g, nxt):
                at = 2 * SA_ * g
                for h in range(H):
                    q_max(g, h)
                    if h:
                        q_low(g, h - 1)
                    if h >= 5:
                        normalise(g, h - 5, at)
                    if h >= 7:
                        mid_low(g, h - 7)
                q_low(g, H - 1)
                mid_low(g, 9)
                cond_low(g + 1, 0)
                cond_low(g + 1, 1)
                normalise(g, 11, at)
                mid_low(g, 10)
                if nxt == 1:
                    late_low(0, 1)
                cond_low(g + 1, 2)
                normalise(g, 12, at)
                mid_low(g, 11)
                if nxt == 1:
                    late_low(1, 2)
                cond_low(g + 1, 3)
                normalise(g, 13, at)
                mid_low(g, 12)
                if nxt == 0:
                    k_bias(g + 1, 0)
                    normalise(g, 14, at)
                    k_max(g + 1, 0)
                    mid_low(g, 13)
                    v_bias(g + 1, 0)
                    normalise(g, 15, at)
                    mid_low(g, 14)
                    add_res(g, 0, 1.0 / (WS * AS))
                    k_bias(g + 1, 1)
                    k_max(g + 1, 1)
                    mid_low(g, 15)
                    v_bias(g + 1, 1)
                    kvprod_low(g + 1, 0)
                    add_res(g, 1, 1.0 / (WS * AS))
                    for p in (2, 3):
                        k_bias(g + 1, p)
                        k_max(g + 1, p)
                        v_bias(g + 1, p)
                        kvprod_low(g + 1, p - 1)
                        if p == 2:
                            add_res(g, p, 1.0 / (WS * AS))
                    kvprod_low(g + 1, 3)
                    add_res(g, 3, 1.0 / (WS * AS))
                else:
                    late_low(2, 3)
                    normalise(g, 14, at)
                    mid_low(g, 13)
                    late_low(3, 4)
                    normalise(g, 15, at)
                    mid_low(g, 14)
                    add_res(g, 0, 1.0 / (WS * AS))
                    late_low(4, 6)
                    mid_low(g, 15)
                    late_low(6, 8)
                    add_res(g, 1, 1.0 / (WS * AS))
                    route(g + 1, 2 * SA_ * NG)
                    late_low(8, 11)
                    add_res(g, 2, 1.0 / (WS * AS))
                    late_low(11, 14)
                    add_res(g, 3, 1.0 / (WS * AS))
                    late_low(14, S_ALL)

            def late_low(v0, v1):
                for v in range(v0, v1):
                    dve.wait_ge(st_hi, v + 1)
                    nc.vector.scalar_tensor_tensor(out=late_unit_at(v, 1), in0=stages[v % 4][:], scalar=WS,
                                                   in1=late_unit_at(v, 0), op0=ALU.mult, op1=ALU.subtract).then_inc(st_lo, 1)

            R_OWN = 3 + 2 * NP + 2

            def route(g, at):
                dve.wait_ge(routed, g - NG + 1)
                nc.vector.scalar_tensor_tensor(out=lg[:], in0=M[:, 0, 0:NP * NB].rearrange("p (a n) -> p a n", a=NP),
                                               scalar=1.0, in1=brb[:].unsqueeze(1).to_broadcast([128, NP, NB]),
                                               op0=ALU.mult, op1=ALU.add).then_inc(lg_read, 1)
                dve.wait_ge(lg_read, g - NG + 1)
                nc.vector.tensor_reduce(mx[:], lg[:], AX.X, ALU.max).then_inc(dve_own, 1)
                dve.wait_ge(dve_own, at + 1)
                nc.vector.tensor_tensor(lg[:], lg[:], mx[:].unsqueeze(2).to_broadcast([128, NP, NB]), ALU.subtract)\
                    .then_inc(dve_own, 1)
                dve.wait_ge(dve_own, at + 2)
                nc.vector.tensor_scalar(lg[:], lg[:], UNDERFLOW, None, ALU.max).then_inc(dve_own, 1)
                dve.wait_ge(dve_own, at + 3)
                nc.vector.memset(pad[:], 0.0)
                for p in range(NP):
                    nc.vector.max(top[:, p, :], lg[:, p, :]).then_inc(dve_own, 1)
                dve.wait_ge(dve_own, at + 3 + NP)
                nc.vector.memset(pad[:], 0.0)
                for p in range(NP):
                    nc.vector.max_index(topi[:, p, :], top[:, p, :], lg[:, p, :]).then_inc(dve_own, 1)
                dve.wait_ge(dve_own, at + 3 + 2 * NP)
                nc.vector.tensor_copy(topf[:], topi[:]).then_inc(dve_own, 1)
                dve.wait_ge(dve_own, at + 4 + 2 * NP)
                for p in range(NP):
                    last = nc.vector.tensor_tensor(eq[:, p, :, :], topf[:, p, 0:TOPK].unsqueeze(2).to_broadcast([128, TOPK, NB]),
                                                   iota[:].unsqueeze(1).to_broadcast([128, TOPK, NB]), ALU.is_equal)
                last.then_inc(dve_own, 1)
                dve.wait_ge(dve_own, at + 5 + 2 * NP)
                nc.vector.tensor_reduce(mask[:], eq.rearrange("p a k n -> p a n k"), AX.X, ALU.add).then_inc(masked, 1)

            def gelu_mask(g, h):
                s = h % 2
                dve.wait_ge(q_free[s], (SQ_ // 2) * g + h // 2 + 2)
                if h % 4 == 0:
                    dve.wait_ge(mask_in[h // 4], 16 * (g - NG + 1))
                nc.vector.tensor_tensor(e[:, s, :], e[:, s, :], maskb[h // 8][:, h % 8, :], ALU.mult).then_inc(e_ready, 1)

            def gelu_low(g, h):
                dve.wait_ge(e_hi, H * g + h + 1)
                nc.vector.tensor_tensor(mid[:, 1, h, :], e[:, h % 2, :], mid[:, 0, h, :], ALU.subtract).then_inc(e_free, 1)

            def body_b(g, more):
                for h in range(H):
                    gelu_mask(g, h)
                    if h:
                        gelu_low(g, h - 1)
                gelu_low(g, H - 1)
                if more:
                    for p in range(NP):
                        cond_low(g + 1, p)
                for p in range(NP):
                    add_res(g, p, 1.0 / WS)
                    if more and p == 0:
                        route(g + 1, 2 * SA_ * NG + R_OWN * (g + 1 - NG))

            def weight_low(v0, v1):
                for v in range(v0, v1):
                    dve.wait_ge(w_hi, v + 1)
                    c = 2 * v % 16
                    nc.vector.scalar_tensor_tensor(out=unit_at(v, 1), in0=wstage[:, c:c + 2, :], scalar=WS,
                                                   in1=unit_at(v, 0), op0=ALU.mult, op1=ALU.subtract).then_inc(w_lo, 1)

            weight_low(0, 2)
            cond_low(0, 0)
            cond_low(0, 1)
            bias_one()
            weight_low(2, 4)
            k_bias(0, 0)
            v_bias(0, 0)
            k_max(0, 0)
            cond_low(0, 2)
            cond_low(0, 3)
            router_low()
            for p in range(1, NP):
                v = W_Q + 4 * (p - 1)
                if p == 1:
                    weight_low(v, v + 2)
                k_bias(0, p)
                if p > 1:
                    weight_low(v, v + 2)
                k_max(0, p)
                if p < 3:
                    weight_low(v + 2, v + 3)
                v_bias(0, p)
                if p < 3:
                    weight_low(v + 3, v + 4)
                kvprod_low(0, p - 1, FIRST)
            weight_low(14, 17)
            kvprod_low(0, 3, FIRST)
            weight_low(17, W_ALL)
            with dve.Fori(0, NG - 1) as g:
                body_a(g, 0)
            body_a(NG - 1, 1)
            with dve.Fori(NG, 2 * NG - 1) as g:
                body_b(g, True)
            body_b(2 * NG - 1, False)

        @block.tensor
        def _(pe):
            pe.sem_inc(heads_free, A_CR)
            pe.sem_inc(t_free, 2)
            pe.sem_inc(o_free, 1)

            def product(out, lhs, rhs, k, n):
                for q, (a, b) in enumerate(PASSES):
                    last = nc.tensor.matmul(out, lhs(a), rhs(b), start=(k == 0 and q == 0),
                                            stop=(k == n - 1 and q == len(PASSES) - 1))
                return last

            def cond(g, p, f, order=STEADY):
                s = p % 2
                pe.wait_ge(x_lo, g * NP + p + 1)
                if order is STEADY:
                    pe.wait_ge(f_read, f + p - 1)
                elif p >= 2:
                    pe.wait_ge(f_read, bank_read(order, "cond", p))
                for k in range(KC):
                    last = product(F[s][:, k * 128:(k + 1) * 128], lambda a: xs[:, s, a, k * 128:(k + 1) * 128],
                                   lambda b: cws[:, s, b, :], 0, 1)
                last.then_inc(cond_done, 1)

            def project(g, p, n, f, order=STEADY):
                pe.wait_ge(f_read, f + max(read(order, "cond", p), bank_read(order, "kv"[n], p)))
                for k in range(KC):
                    last = product(F[n][:], lambda a: hT[:, a, k, p * 128:(p + 1) * 128],
                                   lambda b: (wk, wv)[n][:, b, k, :], k, KC)
                last.then_inc((k_done, v_done)[n], 1)

            def kv_product(g, p, n, f, order=STEADY):
                s, jj, b = p % 2, n // 2, n % 2
                if n == 0:
                    pe.wait_ge(sk_lo, g * NP + p + 1)
                    pe.wait_ge(vs_lo, g * NP + p + 1)
                before = bank_read(order, "kv", p, n)
                if before is not None:
                    pe.wait_ge(f_read, f + before)
                rows = slice(64 * b, 64 * b + 64)
                for t in range(2):
                    j = 2 * jj + t
                    last = product(bank(order, ("kv", p, n))[0][:, t * DV:(t + 1) * DV], lambda a: sk[rows, s, a, j * D:(j + 1) * D],
                                   lambda c: vs[rows, s, c, j, :], 0, 1)
                last.then_inc(kv_done, 1)

            def wide(g, h, w1=False):
                pe.wait_ge(q_free[h % 2], (SQ_ // 2) * g + h // 2 + 1)
                if h % 4 == 0:
                    if w1:
                        pe.wait_ge(st_lo, h // 2 + 2)
                    else:
                        pe.wait_ge(w_lo, W_Q + h // 2 + 2)
                for k in range(KC):
                    last = product(Q[h % 2][:], lambda a: wa[:, a, k, h * D:(h + 1) * D], lambda b: hT[:, b, k, :], k, KC)
                last.then_inc(q_done, 1)

            def heads(g, n):
                j, i = n // NP, n % NP
                pe.wait_ge(e_free, H * g + GQ * j + GQ - 1 + 3)
                pe.wait_ge(m_free, SA_ * g + n + 1)
                for b in range(2):
                    for t in range(2):
                        last = product(M[:, b, t * DV:(t + 1) * DV],
                                       lambda a: sq[:, j % 2, a, 2 * i + b, 2 * t:2 * t + 2, :].rearrange("p h s -> p (h s)"),
                                       lambda c: kv[:, c, 2 * i + b, j, :], 0, 1)
                last.then_inc(heads_free, 1)

            def turn(g, n):
                pe.wait_ge(m_free, SA_ * g + n + 2)
                pe.wait_ge(tr_free, SA_ * g + n + 1)
                for t in range(4):
                    last = nc.tensor.transpose(TR[n % 2][:, t * 128:(t + 1) * 128], att[:, n % 2, t, :], ident[:])
                last.then_inc(t_free, 1)

            def output(g, p, c, w2=False):
                if c == 0:
                    pe.wait_ge(q_free[p % 2], (SQ_ // 2) * g + H // 2 + p // 2 + 1)
                if not w2:
                    pe.wait_ge(w_lo, W_O + 2 * (c + 1))
                    pe.wait_ge(tr_free, SA_ * g + NP * c + p + 3)
                elif p == 0:
                    pe.wait_ge(st_lo, S_1 + 2 * (c + 1))
                    pe.wait_ge(e_free, H * g + 4 * c + 3 + 3)
                for h in range(4 * c, 4 * c + 4):
                    last = product(Q[p % 2][:], lambda a: mid[:, a, h, p * 128:(p + 1) * 128],
                                   lambda b: (w2s[b] if w2 else wb[:, b])[:, h, :], h, H)
                if c == 3:
                    last.then_inc(o_free, 1)

            def router(g):
                if not (isinstance(g, int) and g == NG):
                    pe.wait_ge(lg_read, g - NG)
                else:
                    pe.wait_ge(m_free, SA_ * NG + 1)
                for p in range(NP):
                    for k in range(KC):
                        last = product(M[:, 0, p * NB:(p + 1) * NB], lambda a: hT[:, a, k, p * 128:(p + 1) * 128],
                                       lambda b: wr[:, b, k, :], k, KC)
                last.then_inc(routed, 1)

            def turn_mask(g):
                pe.wait_ge(masked, g - NG + 1)
                if not (isinstance(g, int) and g == NG):
                    pe.wait_ge(maskT_sb, g - NG)
                for p in range(NP):
                    last = nc.tensor.transpose(M[0:NB, 1, p * 128:(p + 1) * 128], mask[:, p, :], ident[:])
                last.then_inc(maskT_ps, 1)

            def body_a(g, nxt, f):
                for h in range(H):
                    wide(g, h)
                    if h == 5:
                        pe.wait_ge(f_read, f)
                    if h >= 5:
                        heads(g, h - 5)
                    if h >= 6:
                        turn(g, h - 6)
                    if h in (13, 14):
                        cond(g + 1, h - 13, f)
                output(g, 0, 0)
                heads(g, 11)
                turn(g, 10)
                output(g, 0, 1)
                cond(g + 1, 2, f)
                heads(g, 12)
                turn(g, 11)
                output(g, 0, 2)
                cond(g + 1, 3, f)
                heads(g, 13)
                turn(g, 12)
                if nxt == 0:
                    project(g + 1, 0, 0, f)
                    heads(g, 14)
                    turn(g, 13)
                    project(g + 1, 0, 1, f)
                    output(g, 0, 3)
                    heads(g, 15)
                    turn(g, 14)
                    project(g + 1, 1, 0, f)
                    turn(g, 15)
                    project(g + 1, 1, 1, f)
                    for p in range(NP):
                        if 0 < p < 3:
                            project(g + 1, p + 1, 0, f)
                            project(g + 1, p + 1, 1, f)
                        for n in range(4):
                            kv_product(g + 1, p, n, f)
                            if p < 3 and (p, n) != (2, 3):
                                output(g, p + 1, n)
                            if (p, n) == (3, 0):
                                output(g, 3, 3)
                else:
                    output(g, 1, 0)
                    heads(g, 14)
                    turn(g, 13)
                    output(g, 0, 3)
                    output(g, 1, 1)
                    heads(g, 15)
                    turn(g, 14)
                    output(g, 1, 2)
                    turn(g, 15)
                    output(g, 1, 3)
                    pe.wait_ge(f_read, f + NP)
                    router(g + 1)
                    for p in (2, 3):
                        for c in range(4):
                            output(g, p, c)
                        if p == 2:
                            turn_mask(g + 1)

            def body_b(g, more, f):
                for h in range(H):
                    wide(g, h, w1=True)
                    if more and h in (13, 14):
                        cond(g + 1, h - 13, f)
                for p in range(NP):
                    for c in range(4):
                        output(g, p, c, w2=True)
                        if more and p == 0 and c in (1, 2):
                            cond(g + 1, 1 + c, f)
                    if more and p == 0:
                        pe.wait_ge(f_read, f + NP)
                        router(g + 1)
                    if more and p == 1:
                        turn_mask(g + 1)

            cond(0, 0, 0, FIRST)
            cond(0, 1, 0, FIRST)
            pe.wait_ge(w_lo, 2)
            project(0, 0, 0, 0, FIRST)
            pe.wait_ge(w_lo, W_Q)
            project(0, 0, 1, 0, FIRST)
            cond(0, 2, 0, FIRST)
            cond(0, 3, 0, FIRST)
            pe.wait_ge(pool_consts, 4)
            pe.wait_ge(dve_consts, 5)
            for p in range(NP):
                if p + 1 < NP:
                    project(0, p + 1, 0, 0, FIRST)
                    project(0, p + 1, 1, 0, FIRST)
                for n in range(4):
                    kv_product(0, p, n, 0, FIRST)
            with pe.Fori(0, NG - 1) as g:
                body_a(g, 0, (g + 1) * SF_)
            body_a(NG - 1, 1, SF_ * NG)
            with pe.Fori(NG, 2 * NG - 1) as g:
                body_b(g, True, SF_ * NG + NP * (g + 1 - NG))
            body_b(2 * NG - 1, False, None)


_SHAPE = (B, C, T)


def kernel(**inputs):
    import numpy as _np
    import concourse.bacc as _bacc
    from concourse import mybir as _mybir
    from concourse.bass_utils import run_bass_kernel_spmd as _run

    nc = _bacc.Bacc("TRN2", target_bir_lowering=False, num_devices=1)
    arr = {k: _np.asarray(v) for k, v in inputs.items()}
    laid = {
        "x": arr["x"], "i1": arr["itok_B_0_7"], "i2": arr["itok_B_1_198"],
        "cw": arr["L0_cond_weights"], "cw2": arr["L0_cond2_weights"],
        "wq": arr["L0_attn_Wq"].T, "wk": arr["L0_attn_Wk"].T, "wv": arr["L0_attn_Wv"].T, "wo": arr["L0_attn_Wo"].T,
        "bq": arr["L0_attn_bq"].reshape(H, D).T, "bk": arr["L0_attn_bk"], "bv": arr["L0_attn_bv"],
        "wr": arr["L0_ffn_Wr"].T, "br": arr["L0_ffn_br"], "w1": arr["L0_ffn_W1"].T, "w2": arr["L0_ffn_W2"].T,
    }
    arrays, args = {}, []
    for name, a in laid.items():
        a = _np.ascontiguousarray(a)
        arrays[f"in_{name}_dram"] = a
        args.append(nc.dram_tensor(f"in_{name}_dram", a.shape, _mybir.dt.from_np(a.dtype), kind="ExternalInput").ap())
    args.append(nc.dram_tensor("x1_dram", _SHAPE, _mybir.dt.float32, kind="Internal").ap())
    args.append(nc.dram_tensor("mask_dram", (NB, TOK), _mybir.dt.float16, kind="Internal").ap())
    args.append(nc.dram_tensor("out_0_dram", _SHAPE, _mybir.dt.float32, kind="ExternalOutput").ap())
    adaln_attn_ffn(nc, *args)
    r = _run(nc, [arrays], core_ids=[0])
    return r.results[0]["out_0_dram"]
```

```python
import concourse.bass as bass
from concourse import mybir
from contextlib import ExitStack

F32 = mybir.dt.float32
F16 = mybir.dt.float16
I32 = mybir.dt.int32
U32 = mybir.dt.uint32
ALU = mybir.AluOpType
ACT = mybir.ActivationFunctionType
AX = mybir.AxisListType

B, C, T = 32, 64, 512
H, KVH, D = 16, 4, 128
GQ = H // KVH
NB, TOPK = 16, 4
KC = T // 128
GB = 8
NG = B // GB
TOK = GB * C
NP = GB // 2
DV = D + 1
WS = 32.0
AS = 16.0
EPS = 1e-6
UNDERFLOW = -104.0
SQ_, SA_, SF_ = H + NP, KVH * NP, NP + 6 * NP
A_CR = 8


def adaln_attn_ffn(nc, x_d, i1_d, i2_d, cw_d, cw2_d, wq_d, wk_d, wv_d, wo_d, bq_d, bk_d, bv_d,
                   wr_d, br_d, w1_d, w2_d, x1_d, mask_d, out_d):
    ctx = ExitStack()
    with ctx:
        def sb(name, shape, dt):
            return ctx.enter_context(nc.sbuf_tensor(name, shape, dt))

        def pb(name):
            return ctx.enter_context(nc.psum_tensor(name, [128, 512], F32))

        def sem(name):
            return ctx.enter_context(nc.semaphore(name))

        wa = sb("wa", [128, 2, KC, H * D], F16)
        wb = sb("wb", [128, 2, H, T], F16)
        wk = sb("wk", [128, 2, KC, KVH * D], F16)
        wv = sb("wv", [128, 2, KC, KVH * D], F16)
        wr = sb("wr", [128, 2, KC, NB], F16)
        wr32 = sb("wr32", [128, KC, NB], F32)
        bq = sb("bq", [128, H], F32)
        bq1 = sb("bq1", [128, H], F32)
        bk1 = sb("bk1", [128, KVH * D], F32)
        bv = sb("bv", [128, KVH * D], F32)
        brb = sb("brb", [128, NB], F32)
        negone = sb("negone", [128, 1], F32)
        zero = sb("zero", [128, 1], F32)
        idx = sb("idx", [1, 2, B], I32)
        ident = sb("ident", [128, 128], F32)
        iota = sb("iota", [128, NB], F32)
        stage = sb("stage", [128, 2, 512], F32)
        xin = sb("xin", [128, 2, T], F32)
        xs = sb("xs", [128, 2, 2, T], F16)
        cw = sb("cw", [128, 2, 128], F32)
        cws = sb("cws", [128, 2, 2, 128], F16)
        hT = sb("hT", [128, 2, KC, TOK], F16)
        ku = sb("ku", [128, KVH * D], F32)
        kvf = sb("kvf", [128, 2, KVH * D], F32)
        kf, vf = kvf[:, 0, :], kvf[:, 1, :]
        sk = sb("sk", [128, 2, 2, KVH * D], F16)
        vs = sb("vs", [128, 2, 2, KVH, DV], F16)
        kv = sb("kv", [128, 2, GB, KVH, DV], F16)
        e = sb("e", [128, 2, TOK], F32)
        u = sb("u", [128, 2, TOK], F32)
        sq = sb("sq", [128, 2, 2, GB, GQ // 2, C, 2], F16)
        att = sb("att", [128, 2, 4, 128], F32)
        att16 = sb("att16", [128, 2, 2, 4, 128], F16)
        den = sb("den", [128, 4], F32)
        rden = sb("rden", [128, 4], F32)
        mids = sb("mids", [128, 2 * H * TOK], F16)
        mid_a = mids[:].rearrange("p (q m n) -> p q m n", q=SA_, m=8)
        mid_h = mids[:].rearrange("p (q a t s h) -> p q a t s h", q=SA_, a=2, t=2, h=2)
        mid = mids[:].rearrange("p (a h t) -> p a h t", a=2, h=H)
        xres = sb("xres", [128, 2, T], F32)
        w2s = (kv[:].rearrange("p a b j d -> p (a b j d)")[:, 0:H * T].rearrange("p (h t) -> p h t", h=H),
               sq[:].rearrange("p s a b t c h -> p (s a b t c h)").rearrange("p (h t) -> p h t", h=H))
        stages = (stage[:], kvf[:], e[:], u[:], att[:].rearrange("p s t d -> p s (t d)"),
                  att16[:].rearrange("p s a t d -> p s (a t d)").bitcast(F32))

        def staged(v):
            b = v if v < 4 else (v - 4) % 6
            return b, v // 4 if v < 4 else (v - 4) // 6 + (b < 4)

        wstage = mids[:].bitcast(F32).rearrange("p (c n) -> p c n", n=512)
        zeros = sq[:].rearrange("p s a b t c h -> p (s a b t c h)")[:, 0:512]
        lg = sb("lg", [128, NP, NB], F32)
        mx = sb("mx", [128, NP], F32)
        top = sb("top", [128, NP, 8], F32)
        topi = sb("topi", [128, NP, 8], U32)
        topf = sb("topf", [128, NP, 8], F32)
        eq = ku[:, 0:NP * TOPK * NB].rearrange("p (a k n) -> p a k n", a=NP, k=TOPK)
        mask = sb("mask", [128, NP, NB], F32)
        pad = sb("pad", [128, 1], F32)
        maskT = sb("maskT", [NB, TOK], F16)
        maskb = tuple(w[:].rearrange("p a k n -> p (a k) n") for w in (wk, wv))

        Q = [pb(f"Q{i}") for i in range(2)]
        F = [pb(f"F{i}") for i in range(2)]
        M = [ctx.enter_context(nc.psum_tensor(f"M{i}", [128, 2, 512], F32)) for i in range(2)]

        idx_in = [sem(f"idx_in{i}") for i in range(2)]
        bias_in = sem("bias_in")
        consts_in = sem("consts_in")
        pool_consts = sem("pool_consts")
        dve_consts = sem("dve_consts")
        zeros_set = sem("zeros_set")
        act_consts = sem("act_consts")
        w_in = [sem(f"w_in{i}") for i in range(4)]
        w_hi = sem("w_hi")
        w_lo = sem("w_lo")
        st_in = [sem(f"st_in{i}") for i in range(6)]
        st_hi = sem("st_hi")
        st_lo = sem("st_lo")
        x_in = [sem(f"x_in{i}") for i in range(2)]
        x_hi = sem("x_hi")
        x_lo = sem("x_lo")
        cond_done = sem("cond_done")
        hT_hi = sem("hT_hi")
        f_read = sem("f_read")
        k_done = sem("k_done")
        v_done = sem("v_done")
        k_exp = sem("k_exp")
        k_elu = sem("k_elu")
        sk_hi = sem("sk_hi")
        sk_lo = sem("sk_lo")
        vs_hi = sem("vs_hi")
        vs_lo = sem("vs_lo")
        kv_done = sem("kv_done")
        kv_hi = sem("kv_hi")
        q_done = sem("q_done")
        q_free = [sem(f"q_free{i}") for i in range(2)]
        e_ready = sem("e_ready")
        e_hi = sem("e_hi")
        e_free = sem("e_free")
        heads_free = sem("heads_free")
        m_free = sem("m_free")
        att_hi = sem("att_hi")
        att_lo = sem("att_lo")
        turns = sem("turns")
        turned = [sem(f"turned{i}") for i in range(2)]
        o_free = sem("o_free")
        res_in = [sem(f"res_in{i}") for i in range(2)]
        stored = [sem(f"stored{i}") for i in range(2)]
        routed = sem("routed")
        lg_read = sem("lg_read")
        dve_own = sem("dve_own")
        masked = sem("masked")
        maskT_ps = sem("maskT_ps")
        maskT_sb = sem("maskT_sb")
        mask_out = sem("mask_out")
        mask_in = [sem(f"mask_in{i}") for i in range(4)]

        CONDS = [("cond", p, 0) for p in range(NP)]
        KVS = [("kv", p, n) for p in range(NP) for n in range(4)]
        PROJ = [(w, p, 0) for p in range(NP) for w in ("k", "v")]
        STEADY = CONDS + PROJ[:4] + KVS[:4] + PROJ[4:6] + KVS[4:8] + PROJ[6:8] + KVS[8:]
        FIRST = CONDS[:2] + PROJ[:2] + CONDS[2:] + STEADY[6:]

        def bank(order, use):
            kind, p, n = use
            if kind == "kv" and order is FIRST:
                return M[n // 2][:, n % 2, :], 2 + n
            i = {"cond": p % 2, "k": 0, "v": 1, "kv": n % 2}[kind]
            return F[i], i

        def read(order, kind, p, n=0):
            return order.index((kind, p, n)) + 1

        def bank_read(order, kind, p, n=0):
            at = order.index((kind, p, n))
            same = [i for i in range(at) if bank(order, order[i])[1] == bank(order, order[at])[1]]
            return same[-1] + 1 if same else None

        UNITS = [(w, k, 0) for w in range(2) for k in range(0, KC, 2)]
        UNITS += [(2, k, j) for j in range(KVH) for k in range(0, KC, 2)] + [(3, h, 0) for h in range(0, H, 2)]
        W_Q, W_O, W_ALL = 4, 12, 20
        S_1, S_ALL = 8, 16

        def unit_at(v, part):
            w, rows, cols = UNITS[v]
            if w == 3:
                return wb[:, part, rows:rows + 2, :]
            return (wk, wv, wa)[w][:, part, rows:rows + 2, cols * 512:(cols + 1) * 512]

        def late_unit_at(v, part):
            if v < S_1:
                return wa[:, part, 2 * (v % 2):2 * (v % 2) + 2, v // 2 * 512:(v // 2 + 1) * 512]
            return w2s[part][:, 2 * (v - S_1):2 * (v - S_1) + 2, :]

        PASSES = ((0, 0), (0, 1), (1, 0))

        block = ctx.enter_context(nc.Block())

        @block.sync
        def _(sp):
            for q in stored:
                sp.sem_inc(q, 16)
            sp.dma_start(idx[0:1, 0, :], i1_d.rearrange("(a n) -> a n", a=1)).then_inc(idx_in[0], 16)

            def load_x(g, p, layer):
                s = p % 2
                src, w_d, n = (x_d, cw_d, 8) if layer == 0 else (x1_d, cw2_d, 200)
                t = (g - NG * layer) * GB + 2 * p
                if not (isinstance(g, int) and g == 0 and p < 2):
                    sp.wait_ge(x_lo, g * NP + p - 1)
                if layer == 1:
                    sp.wait_ge(stored[s], 16 * (2 * (g - NG) + p // 2 + 2))
                sp.dma_start(xin[:, s, :], src[bass.ds(t, 2), :, :].rearrange("b c t -> (b c) t")).then_inc(x_in[s], 16)
                if isinstance(g, int) and g == 0 and p == 0:
                    sp.wait_ge(idx_in[0], 16)
                    sp.wait_ge(pool_consts, 1)
                for h in range(2):
                    if h == 1 and isinstance(g, int) and g == 0 and p < 2:
                        break
                    i = sp.value_load(idx[0:1, layer, bass.ds(t + h, 1)], min_val=0, max_val=n - 1)
                    sp.dma_start(cw[64 * h:64 * h + 64, s, 64 * h:64 * h + 64],
                                 w_d[bass.ds(i, 1), :, :].rearrange("a c d -> (a c) d")).then_inc(x_in[s], 16)

            def load_res(g, p, layer):
                s = p % 2
                t = (g - NG * layer) * GB + 2 * p
                sp.wait_ge(stored[s], 16 * (2 * g + p // 2 + 1))
                sp.dma_start(xres[:, s, :], (x1_d if layer else x_d)[bass.ds(t, 2), :, :]
                             .rearrange("b c t -> (b c) t")).then_inc(res_in[s], 16)

            def store(g, p, layer):
                s = p % 2
                t = (g - NG * layer) * GB + 2 * p
                sp.wait_ge(q_free[s], (SQ_ // 2) * g + H // 2 + p // 2 + 2)
                sp.dma_start((out_d if layer else x1_d)[bass.ds(t, 2), :, :]
                             .rearrange("b c t -> (b c) t"), xres[:, s, :]).then_inc(stored[s], 16)

            def body(g, layer, nxt):
                if nxt is not None:
                    load_x(g + 1, 0, nxt)
                    load_x(g + 1, 1, nxt)
                load_res(g, 0, layer)
                load_res(g, 1, layer)
                if nxt is not None:
                    load_x(g + 1, 2, nxt)
                    load_x(g + 1, 3, nxt)
                store(g, 0, layer)
                load_res(g, 2, layer)
                store(g, 1, layer)
                load_res(g, 3, layer)
                store(g, 2, layer)
                store(g, 3, layer)

            def load_weights(q):
                w, rows, cols = UNITS[2 * q]
                w_d = (wk_d, wv_d, wq_d, wo_d)[w]
                if q >= 4:
                    sp.wait_ge(w_lo, 2 * (q - 3))
                sp.dma_start(wstage[:, 4 * (q % 4):4 * (q % 4) + 4, :],
                             w_d[rows * 128:(rows + 4) * 128, cols * 512:(cols + 1) * 512]
                             .rearrange("(k p) n -> p k n", p=128)).then_inc(w_in[q % 4], 16)

            load_x(0, 0, 0)
            load_x(0, 1, 0)
            load_weights(1)
            for n, (b_sb, b_d) in enumerate(((bk1, bk_d), (bv, bv_d))):
                sp.dma_start(b_sb[:], b_d.rearrange("(a n) -> a n", a=1).to_broadcast([128, 512])).then_inc(bias_in, 16)
                load_x(0, 2 + n, 0)
            sp.dma_start(bq[:], bq_d).then_inc(consts_in, 16)
            sp.dma_start(brb[:], br_d.rearrange("(a n) -> a n", a=1).to_broadcast([128, NB])).then_inc(consts_in, 16)
            sp.dma_start(wr32[:], wr_d.rearrange("(k p) n -> p k n", p=128)).then_inc(consts_in, 16)
            for q in range(2, 10):
                load_weights(q)
            sp.dma_start(idx[0:1, 1, :], i2_d.rearrange("(a n) -> a n", a=1)).then_inc(idx_in[1], 16)
            sp.wait_ge(idx_in[1], 16)
            body(0, 0, 0)
            with sp.Fori(1, NG - 1) as g:
                body(g, 0, 0)
            body(NG - 1, 0, 1)
            with sp.Fori(NG, 2 * NG - 1) as g:
                body(g, 1, 1)
            body(2 * NG - 1, 1, None)
            for q in stored:
                sp.wait_ge(q, 16 * (4 * NG + 1))

        @block.gpsimd
        def _(pool):
            pool.memset(cw[:], 0.0).then_inc(pool_consts, 1)
            pool.memset(ident[:], 0.0).then_inc(pool_consts, 1)
            pool.iota(iota[:], pattern=[[1, NB]], base=0, channel_multiplier=0,
                      allow_small_or_imprecise_dtypes=True).then_inc(pool_consts, 1)
            pool.wait_ge(pool_consts, 3)
            pool.affine_select(out=ident[:], in_=ident[:], compare_op=ALU.not_equal, fill=1.0, base=0,
                               pattern=[[-1, 128]], channel_multiplier=1).then_inc(pool_consts, 1)

            def x_split(g, p):
                s = p % 2
                pool.wait_ge(x_hi, g * NP + p + 1)
                pool.tensor_tensor(xs[:, s, 1, :], xin[:, s, :], xs[:, s, 0, :], ALU.subtract)
                pool.tensor_tensor(cws[:, s, 1, :], cw[:, s, :], cws[:, s, 0, :], ALU.subtract).then_inc(x_lo, 1)

            def kv_split(g, p):
                s = p % 2
                pool.wait_ge(sk_hi, g * NP + p + 1)
                pool.tensor_tensor(sk[:, s, 1, :], kf, sk[:, s, 0, :], ALU.subtract).then_inc(sk_lo, 1)
                pool.wait_ge(vs_hi, g * NP + p + 1)
                pool.tensor_tensor(vs[:, s, 1, :, 0:D], vf.rearrange("p (h d) -> p h d", h=KVH),
                                   vs[:, s, 0, :, 0:D], ALU.subtract).then_inc(vs_lo, 1)

            x_split(0, 0)
            x_split(0, 1)
            x_split(0, 2)
            x_split(0, 3)
            for p in range(NP):
                kv_split(0, p)
            with pool.Fori(0, NG - 1) as g:
                for p in range(NP):
                    x_split(g + 1, p)
                for p in range(NP):
                    kv_split(g + 1, p)
            for p in range(NP):
                x_split(NG, p)
            with pool.Fori(NG, 2 * NG - 1) as g:
                for p in range(NP):
                    x_split(g + 1, p)

        @block.scalar
        def _(act):
            act.wait_ge(dve_consts, 1)
            nc.scalar.activation(bq1[:, 0:1], negone[:], ACT.Exp)
            act.wait_ge(idx_in[0], 16)
            act.wait_ge(pool_consts, 1)
            for p in range(2):
                i = act.value_load(idx[0:1, 0, 2 * p + 1:2 * p + 2], min_val=0, max_val=7)
                act.dma_start(cw[64:128, p, 64:128], cw_d[bass.ds(i, 1), :, :].rearrange("a c d -> (a c) d"))\
                    .then_inc(x_in[p], 16)
            act.dma_start(wstage[:, 0:4, :], wk_d.rearrange("(k p) n -> p k n", p=128)).then_inc(w_in[0], 16)

            def constants():
                act.wait_ge(consts_in, 48)
                act.wait_ge(dve_consts, 3)
                nc.scalar.activation(bq1[:], bq[:], ACT.Identity, bias=1.0).then_inc(act_consts, 1)
                nc.scalar.activation(wr[:, 0, :, :], wr32[:], ACT.Copy).then_inc(act_consts, 1)

            def x_high(g, p):
                s = p % 2
                act.wait_ge(x_in[s], 48 * (2 * g + p // 2 + 1))
                if not (isinstance(g, int) and g == 0 and p < 2):
                    act.wait_ge(cond_done, g * NP + p - 1)
                nc.scalar.activation(xs[:, s, 0, :], xin[:, s, :], ACT.Copy)
                nc.scalar.activation(cws[:, s, 0, :], cw[:, s, :], ACT.Copy).then_inc(x_hi, 1)

            def cond_high(g, p):
                act.wait_ge(cond_done, g * NP + p + 1)
                if not (isinstance(g, int) and g == 0):
                    act.wait_ge(q_done, H * g)
                nc.scalar.activation(hT[:, 0, :, p * 128:(p + 1) * 128], F[p % 2][:].rearrange("p (k n) -> p k n", k=KC),
                                     ACT.Copy).then_inc(hT_hi, 1)

            def k_expo(g, p, f, order=STEADY):
                act.wait_ge(f_read, f + read(order, "k", p))
                if not (isinstance(g, int) and g == 0 and p == 0):
                    act.wait_ge(sk_lo, g * NP + p)
                nc.scalar.activation(kf, ku[:], ACT.Exp, bias=negone[:]).then_inc(k_exp, 1)

            def k_high(g, p):
                s = p % 2
                act.wait_ge(k_elu, g * NP + p + 1)
                if not (isinstance(g, int) and g == 0 and p < 2):
                    act.wait_ge(kv_done, 4 * (g * NP + p - 1))
                nc.scalar.activation(sk[:, s, 0, :], kf, ACT.Copy).then_inc(sk_hi, 1)

            def v_high(g, p, f, order=STEADY):
                s = p % 2
                act.wait_ge(f_read, f + read(order, "v", p))
                nc.scalar.activation(vs[:, s, 0, :, 0:D], vf.rearrange("p (h d) -> p h d", h=KVH),
                                     ACT.Copy).then_inc(vs_hi, 1)

            def kvprod_high(g, p, order=STEADY):
                for n in range(4):
                    jj, b = n // 2, n % 2
                    act.wait_ge(kv_done, 4 * (g * NP + p) + n + 1)
                    act.wait_ge(heads_free, SA_ * g + A_CR)
                    nc.scalar.activation(kv[:, 0, 2 * p + b, 2 * jj:2 * jj + 2, :],
                                         bank(order, ("kv", p, n))[0][:, 0:2 * DV].rearrange("p (j d) -> p j d", j=2), ACT.Copy).then_inc(kv_hi, 1)

            def q_read(g, h):
                s = h % 2
                act.wait_ge(q_done, H * g + h + 1)
                act.wait_ge(e_free, H * g + h + 1)
                nc.scalar.activation(e[:, s, :], Q[s][:], ACT.Exp, bias=bq[:, h:h + 1], scale=1.0 / WS)
                nc.scalar.activation(u[:, s, :], Q[s][:], ACT.Identity, bias=bq1[:, h:h + 1],
                                     scale=1.0 / WS).then_inc(q_free[s], 1)

            def q_high(g, h):
                act.wait_ge(e_ready, H * g + h + 1)
                act.wait_ge(heads_free, SA_ * g + 4 * (h // GQ) - 4 + A_CR)
                nc.scalar.activation(sq[:, (h // GQ) % 2, 0, :, h % GQ // 2, :, h % 2],
                                     e[:, h % 2, :].rearrange("p (b s) -> p b s", b=GB), ACT.Copy).then_inc(e_hi, 1)

            def att_high(g, n):
                s = n % 2
                act.wait_ge(m_free, SA_ * g + n + 3)
                if not (isinstance(g, int) and g == 0 and n < 2):
                    act.wait_ge(turned[s], 16 * SA_ // 2 * g + 16 * (n // 2))
                nc.scalar.activation(att16[:, s, 0, :, :], att[:, s, :, :], ACT.Copy).then_inc(att_hi, 1)

            def turn(g, n):
                act.wait_ge(att_lo, SA_ * g + n + 1)
                act.wait_ge(o_free, NP * g + 1)
                act.sem_inc(turns, 1)
                act.dma_start_transpose(mid_a[:, n, :, :], att16[:, n % 2, :, :, :].rearrange("p a t d -> p (a t d)"))\
                    .then_inc(turned[n % 2], 16)

            def fetch(v):
                if v >= S_ALL:
                    return
                b, use = staged(v)
                if use:
                    act.wait_ge(st_lo, max(w for w in range(v) if staged(w)[0] == b) + 1)
                elif b == 1:
                    act.wait_ge(sk_lo, NP * NG)
                    act.wait_ge(vs_lo, NP * NG)
                elif b in (2, 3):
                    act.wait_ge(e_free, H * NG + 2)
                elif b == 4:
                    act.wait_ge(att_lo, SA_ * NG)
                elif b == 5:
                    for q in turned:
                        act.wait_ge(q, 16 * SA_ // 2 * NG)
                w_d, rows, cols = (w1_d, 2 * (v % 2), v // 2) if v < S_1 else (w2_d, 2 * (v - S_1), 0)
                act.dma_start(stages[b], w_d[rows * 128:(rows + 2) * 128, cols * 512:(cols + 1) * 512]
                              .rearrange("(k p) n -> p k n", p=128)).then_inc(st_in[b], 16)

            def late_high(v0, v1):
                for v in range(v0, v1):
                    if 1 <= v < 5:
                        fetch(v + 3)
                    elif v > 5:
                        fetch(v + 4)
                    b, use = staged(v)
                    act.wait_ge(st_in[b], 16 * (use + 1))
                    if v == 0:
                        act.wait_ge(q_done, H * NG)
                    if v == S_1:
                        act.wait_ge(heads_free, SA_ * NG + A_CR)
                    nc.scalar.activation(late_unit_at(v, 0), stages[b], ACT.Copy, scale=WS).then_inc(st_hi, 1)

            def body_a(g, nxt, f):
                if nxt == 1:
                    fetch(0)
                    fetch(1)
                for h in range(H):
                    q_read(g, h)
                    if h:
                        q_high(g, h - 1)
                    if isinstance(g, int) and g == 0 and h < W_ALL - W_O:
                        weight_high(W_O + h, W_O + h + 1)
                    if h >= 6:
                        att_high(g, h - 6)
                    if h >= 7:
                        turn(g, h - 7)
                    if h in (8, 9):
                        x_high(g + 1, h - 8)
                    if h == 14:
                        x_high(g + 1, 2)
                    if h == 15:
                        x_high(g + 1, 3)
                q_high(g, H - 1)
                turn(g, 9)
                cond_high(g + 1, 0)
                cond_high(g + 1, 1)
                att_high(g, 10)
                if nxt == 1:
                    fetch(2)
                    fetch(3)
                turn(g, 10)
                att_high(g, 11)
                cond_high(g + 1, 2)
                turn(g, 11)
                att_high(g, 12)
                cond_high(g + 1, 3)
                if nxt == 0:
                    turn(g, 12)
                    att_high(g, 13)
                    k_expo(g + 1, 0, f)
                    att_high(g, 14)
                    turn(g, 13)
                    k_high(g + 1, 0)
                    v_high(g + 1, 0, f)
                    att_high(g, 15)
                    turn(g, 14)
                    k_expo(g + 1, 1, f)
                    turn(g, 15)
                    k_high(g + 1, 1)
                    v_high(g + 1, 1, f)
                    kvprod_high(g + 1, 0)
                    for p in (2, 3):
                        k_expo(g + 1, p, f)
                        k_high(g + 1, p)
                        v_high(g + 1, p, f)
                        kvprod_high(g + 1, p - 1)
                    kvprod_high(g + 1, 3)
                else:
                    late_high(0, 1)
                    att_high(g, 13)
                    turn(g, 12)
                    late_high(1, 2)
                    att_high(g, 14)
                    turn(g, 13)
                    late_high(2, 3)
                    att_high(g, 15)
                    turn(g, 14)
                    late_high(3, 4)
                    turn(g, 15)
                    fetch(8)
                    fetch(9)
                    late_high(4, 11)
                    mask_high(g + 1)
                    late_high(11, 14)
                    mask_broadcast(g + 1)
                    late_high(14, S_ALL)
                    act.wait_ge(st_lo, S_ALL)

            def mask_high(g):
                act.wait_ge(maskT_ps, g - NG + 1)
                if not (isinstance(g, int) and g == NG):
                    act.wait_ge(mask_out, 16 * (g - NG))
                nc.scalar.activation(maskT[:], M[0][0:NB, 1, :], ACT.Copy).then_inc(maskT_sb, 1)
                act.wait_ge(maskT_sb, g - NG + 1)
                act.wait_ge(e_ready, H * g)
                act.dma_start(mask_d, maskT[:]).then_inc(mask_out, 16)

            def mask_broadcast(g):
                act.wait_ge(mask_out, 16 * (g - NG + 1))
                for q in range(4):
                    act.dma_start(maskb[q // 2][:, q % 2 * 4:q % 2 * 4 + 4, :].rearrange("p n t -> p (n t)"),
                                  mask_d[4 * q:4 * q + 4, :].rearrange("(a n) t -> a (n t)", a=1)
                                  .to_broadcast([128, 4 * TOK])).then_inc(mask_in[q], 16)

            def gelu_read(g, h):
                s = h % 2
                act.wait_ge(q_done, H * g + h + 1)
                act.wait_ge(e_free, H * g + h + 1)
                nc.scalar.activation(e[:, s, :], Q[s][:], ACT.Gelu, bias=zero[:], scale=1.0 / WS).then_inc(q_free[s], 1)

            def gelu_high(g, h):
                act.wait_ge(e_ready, H * g + h + 1)
                act.wait_ge(o_free, NP * g + 1)
                nc.scalar.activation(mid[:, 0, h, :], e[:, h % 2, :], ACT.Copy).then_inc(e_hi, 1)

            def body_b(g, more):
                for h in range(H):
                    gelu_read(g, h)
                    if h:
                        gelu_high(g, h - 1)
                    if more and h in (8, 9):
                        x_high(g + 1, h - 8)
                    if more and h in (14, 15):
                        x_high(g + 1, h - 12)
                gelu_high(g, H - 1)
                if more:
                    for p in range(NP):
                        cond_high(g + 1, p)
                    mask_high(g + 1)
                    mask_broadcast(g + 1)

            def weight_high(v0, v1):
                for v in range(v0, v1):
                    act.wait_ge(w_in[v // 2 % 4], 16 * (v // 8 + 1))
                    c = 2 * v % 16
                    nc.scalar.activation(unit_at(v, 0), wstage[:, c:c + 2, :], ACT.Copy, scale=WS).then_inc(w_hi, 1)

            x_high(0, 0)
            x_high(0, 1)
            weight_high(0, 2)
            cond_high(0, 0)
            cond_high(0, 1)
            weight_high(2, 4)
            x_high(0, 2)
            x_high(0, 3)
            k_expo(0, 0, 0, FIRST)
            cond_high(0, 2)
            cond_high(0, 3)
            k_high(0, 0)
            v_high(0, 0, 0, FIRST)
            constants()
            for p in range(1, NP):
                v = W_Q + 3 * (p - 1)
                if p < 3:
                    weight_high(v, v + 1)
                k_expo(0, p, 0, FIRST)
                if p < 3:
                    weight_high(v + 1, v + 2)
                k_high(0, p)
                if p < 3:
                    weight_high(v + 2, v + 3)
                v_high(0, p, 0, FIRST)
                kvprod_high(0, p - 1, FIRST)
            weight_high(10, W_O)
            kvprod_high(0, 3, FIRST)
            body_a(0, 0, SF_)
            with act.Fori(1, NG - 1) as g:
                body_a(g, 0, (g + 1) * SF_)
            body_a(NG - 1, 1, SF_ * NG)
            with act.Fori(NG, 2 * NG - 1) as g:
                body_b(g, True)
            body_b(2 * NG - 1, False)

        @block.vector
        def _(dve):
            for q in q_free:
                dve.sem_inc(q, 1)
            dve.sem_inc(e_free, 2)
            dve.sem_inc(m_free, 2)
            nc.vector.memset(zeros, 0.0).then_inc(zeros_set, 1)
            nc.vector.memset(negone[:], -1.0).then_inc(dve_consts, 1)
            nc.vector.memset(zero[:], 0.0).then_inc(dve_consts, 1)
            for s in range(2):
                nc.vector.memset(vs[:, s, 0, :, D:DV], 1.0)
                last = nc.vector.memset(vs[:, s, 1, :, D:DV], 0.0)
            last.then_inc(dve_consts, 1)

            def bias_one():
                dve.wait_ge(bias_in, 32)
                nc.vector.tensor_scalar(bk1[:], bk1[:], 1.0, None, ALU.add).then_inc(dve_consts, 1)
                dve.wait_ge(dve_consts, 4)

            def router_low():
                dve.wait_ge(act_consts, 2)
                nc.vector.tensor_tensor(wr[:, 1, :, :], wr32[:], wr[:, 0, :, :], ALU.subtract).then_inc(dve_consts, 1)

            def cond_low(g, p):
                dve.wait_ge(hT_hi, g * NP + p + 1)
                nc.vector.tensor_tensor(hT[:, 1, :, p * 128:(p + 1) * 128], F[p % 2][:].rearrange("p (k n) -> p k n", k=KC),
                                        hT[:, 0, :, p * 128:(p + 1) * 128], ALU.subtract).then_inc(f_read, 1)

            def k_bias(g, p):
                dve.wait_ge(k_done, g * NP + p + 1)
                nc.vector.scalar_tensor_tensor(out=ku[:], in0=F[0][:], scalar=1.0 / WS, in1=bk1[:],
                                               op0=ALU.mult, op1=ALU.add).then_inc(f_read, 1)

            def v_bias(g, p):
                dve.wait_ge(v_done, g * NP + p + 1)
                if not (isinstance(g, int) and g == 0 and p == 0):
                    dve.wait_ge(vs_lo, g * NP + p)
                nc.vector.scalar_tensor_tensor(out=vf, in0=F[1][:], scalar=1.0 / WS, in1=bv[:],
                                               op0=ALU.mult, op1=ALU.add).then_inc(f_read, 1)

            def k_max(g, p):
                dve.wait_ge(k_exp, g * NP + p + 1)
                nc.vector.scalar_tensor_tensor(out=kf, in0=kf, scalar=1.0, in1=ku[:],
                                               op0=ALU.min, op1=ALU.max).then_inc(k_elu, 1)

            def kvprod_low(g, p, order=STEADY):
                for n in range(4):
                    jj, b = n // 2, n % 2
                    dve.wait_ge(kv_hi, 4 * (g * NP + p) + n + 1)
                    nc.vector.tensor_tensor(kv[:, 1, 2 * p + b, 2 * jj:2 * jj + 2, :],
                                            bank(order, ("kv", p, n))[0][:, 0:2 * DV].rearrange("p (j d) -> p j d", j=2),
                                            kv[:, 0, 2 * p + b, 2 * jj:2 * jj + 2, :], ALU.subtract).then_inc(f_read, 1)

            def q_max(g, h):
                s = h % 2
                dve.wait_ge(q_free[s], (SQ_ // 2) * g + h // 2 + 2)
                nc.vector.scalar_tensor_tensor(out=e[:, s, :], in0=e[:, s, :], scalar=1.0, in1=u[:, s, :],
                                               op0=ALU.min, op1=ALU.max).then_inc(e_ready, 1)

            def q_low(g, h):
                dve.wait_ge(e_hi, H * g + h + 1)
                nc.vector.tensor_tensor(sq[:, (h // GQ) % 2, 1, :, h % GQ // 2, :, h % 2],
                                        e[:, h % 2, :].rearrange("p (b s) -> p b s", b=GB),
                                        sq[:, (h // GQ) % 2, 0, :, h % GQ // 2, :, h % 2], ALU.subtract).then_inc(e_free, 1)

            def normalise(g, n, at):
                dve.wait_ge(heads_free, SA_ * g + n + 1 + A_CR)
                Mq = M[n % 2]
                nc.vector.tensor_scalar(den[:].rearrange("p (a b) -> p a b", a=2), Mq[:, :, D:2 * DV:DV], EPS, 1.0 / AS,
                                        ALU.add, ALU.mult).then_inc(dve_own, 1)
                dve.wait_ge(dve_own, at + 2 * n + 1)
                nc.vector.reciprocal(rden[:], den[:]).then_inc(dve_own, 1)
                dve.wait_ge(dve_own, at + 2 * n + 2)
                nc.vector.tensor_tensor(att[:, n % 2, :, :].rearrange("p (b a) d -> p a b d", a=2),
                                        Mq[:, :, 0:2 * DV].rearrange("p a (b d) -> p a b d", b=2)[:, :, :, 0:D],
                                        rden[:].rearrange("p (a b) -> p a b", a=2).unsqueeze(3).to_broadcast([128, 2, 2, D]),
                                        ALU.mult).then_inc(m_free, 1)

            def att_low(g, n):
                s = n % 2
                dve.wait_ge(att_hi, SA_ * g + n + 1)
                nc.vector.tensor_tensor(att16[:, s, 1, :, :], att[:, s, :, :], att16[:, s, 0, :, :],
                                        ALU.subtract).then_inc(att_lo, 1)

            def add_res(g, p, scale):
                s = p % 2
                dve.wait_ge(o_free, NP * g + p + 2)
                dve.wait_ge(res_in[s], 16 * (2 * g + p // 2 + 1))
                nc.vector.scalar_tensor_tensor(out=xres[:, s, :], in0=Q[s][:], scalar=scale, in1=xres[:, s, :],
                                               op0=ALU.mult, op1=ALU.add).then_inc(q_free[s], 1)

            def body_a(g, nxt):
                at = 2 * SA_ * g
                for h in range(H):
                    q_max(g, h)
                    if h:
                        q_low(g, h - 1)
                    if isinstance(g, int) and g == 0 and h < W_ALL - W_O:
                        weight_low(W_O + h, W_O + h + 1)
                    if h >= 5:
                        normalise(g, h - 5, at)
                    if h >= 6:
                        att_low(g, h - 6)
                q_low(g, H - 1)
                cond_low(g + 1, 0)
                cond_low(g + 1, 1)
                att_low(g, 10)
                normalise(g, 11, at)
                att_low(g, 11)
                normalise(g, 12, at)
                cond_low(g + 1, 2)
                att_low(g, 12)
                normalise(g, 13, at)
                cond_low(g + 1, 3)
                if nxt == 0:
                    k_bias(g + 1, 0)
                    att_low(g, 13)
                    normalise(g, 14, at)
                    k_max(g + 1, 0)
                    v_bias(g + 1, 0)
                    att_low(g, 14)
                    normalise(g, 15, at)
                    k_bias(g + 1, 1)
                    att_low(g, 15)
                    k_max(g + 1, 1)
                    add_res(g, 0, 1.0 / (WS * AS))
                    v_bias(g + 1, 1)
                    kvprod_low(g + 1, 0)
                    add_res(g, 1, 1.0 / (WS * AS))
                    for p in (2, 3):
                        k_bias(g + 1, p)
                        k_max(g + 1, p)
                        v_bias(g + 1, p)
                        kvprod_low(g + 1, p - 1)
                        if p == 2:
                            add_res(g, p, 1.0 / (WS * AS))
                    kvprod_low(g + 1, 3)
                    add_res(g, 3, 1.0 / (WS * AS))
                else:
                    late_low(0, 1)
                    att_low(g, 13)
                    normalise(g, 14, at)
                    late_low(1, 2)
                    att_low(g, 14)
                    normalise(g, 15, at)
                    late_low(2, 3)
                    att_low(g, 15)
                    late_low(3, 4)
                    add_res(g, 0, 1.0 / (WS * AS))
                    late_low(4, 6)
                    add_res(g, 1, 1.0 / (WS * AS))
                    route(g + 1, 2 * SA_ * NG)
                    late_low(6, 10)
                    add_res(g, 2, 1.0 / (WS * AS))
                    late_low(10, 14)
                    add_res(g, 3, 1.0 / (WS * AS))
                    late_low(14, S_ALL)

            def late_low(v0, v1):
                for v in range(v0, v1):
                    dve.wait_ge(st_hi, v + 1)
                    nc.vector.scalar_tensor_tensor(out=late_unit_at(v, 1), in0=stages[staged(v)[0]], scalar=WS,
                                                   in1=late_unit_at(v, 0), op0=ALU.mult, op1=ALU.subtract).then_inc(st_lo, 1)

            R_OWN = 3 + 2 * NP + 2

            def route(g, at):
                dve.wait_ge(routed, g - NG + 1)
                nc.vector.scalar_tensor_tensor(out=lg[:], in0=M[0][:, 0, 0:NP * NB].rearrange("p (a n) -> p a n", a=NP),
                                               scalar=1.0, in1=brb[:].unsqueeze(1).to_broadcast([128, NP, NB]),
                                               op0=ALU.mult, op1=ALU.add).then_inc(lg_read, 1)
                dve.wait_ge(lg_read, g - NG + 1)
                nc.vector.tensor_reduce(mx[:], lg[:], AX.X, ALU.max).then_inc(dve_own, 1)
                dve.wait_ge(dve_own, at + 1)
                nc.vector.tensor_tensor(lg[:], lg[:], mx[:].unsqueeze(2).to_broadcast([128, NP, NB]), ALU.subtract)\
                    .then_inc(dve_own, 1)
                dve.wait_ge(dve_own, at + 2)
                nc.vector.tensor_scalar(lg[:], lg[:], UNDERFLOW, None, ALU.max).then_inc(dve_own, 1)
                dve.wait_ge(dve_own, at + 3)
                nc.vector.memset(pad[:], 0.0)
                for p in range(NP):
                    nc.vector.max(top[:, p, :], lg[:, p, :]).then_inc(dve_own, 1)
                dve.wait_ge(dve_own, at + 3 + NP)
                nc.vector.memset(pad[:], 0.0)
                for p in range(NP):
                    nc.vector.max_index(topi[:, p, :], top[:, p, :], lg[:, p, :]).then_inc(dve_own, 1)
                dve.wait_ge(dve_own, at + 3 + 2 * NP)
                nc.vector.tensor_copy(topf[:], topi[:]).then_inc(dve_own, 1)
                dve.wait_ge(dve_own, at + 4 + 2 * NP)
                for p in range(NP):
                    last = nc.vector.tensor_tensor(eq[:, p, :, :], topf[:, p, 0:TOPK].unsqueeze(2).to_broadcast([128, TOPK, NB]),
                                                   iota[:].unsqueeze(1).to_broadcast([128, TOPK, NB]), ALU.is_equal)
                last.then_inc(dve_own, 1)
                dve.wait_ge(dve_own, at + 5 + 2 * NP)
                nc.vector.tensor_reduce(mask[:], eq.rearrange("p a k n -> p a n k"), AX.X, ALU.add).then_inc(masked, 1)

            def gelu_mask(g, h):
                s = h % 2
                dve.wait_ge(q_free[s], (SQ_ // 2) * g + h // 2 + 2)
                if h % 4 == 0:
                    dve.wait_ge(mask_in[h // 4], 16 * (g - NG + 1))
                nc.vector.tensor_tensor(e[:, s, :], e[:, s, :], maskb[h // 8][:, h % 8, :], ALU.mult).then_inc(e_ready, 1)

            def gelu_low(g, h):
                dve.wait_ge(e_hi, H * g + h + 1)
                nc.vector.tensor_tensor(mid[:, 1, h, :], e[:, h % 2, :], mid[:, 0, h, :], ALU.subtract).then_inc(e_free, 1)

            def body_b(g, more):
                for h in range(H):
                    gelu_mask(g, h)
                    if h:
                        gelu_low(g, h - 1)
                gelu_low(g, H - 1)
                if more:
                    for p in range(NP):
                        cond_low(g + 1, p)
                for p in range(NP):
                    add_res(g, p, 1.0 / WS)
                    if more and p == 0:
                        route(g + 1, 2 * SA_ * NG + R_OWN * (g + 1 - NG))

            def weight_low(v0, v1):
                for v in range(v0, v1):
                    dve.wait_ge(w_hi, v + 1)
                    c = 2 * v % 16
                    nc.vector.scalar_tensor_tensor(out=unit_at(v, 1), in0=wstage[:, c:c + 2, :], scalar=WS,
                                                   in1=unit_at(v, 0), op0=ALU.mult, op1=ALU.subtract).then_inc(w_lo, 1)

            weight_low(0, 2)
            cond_low(0, 0)
            cond_low(0, 1)
            bias_one()
            weight_low(2, 4)
            k_bias(0, 0)
            v_bias(0, 0)
            k_max(0, 0)
            cond_low(0, 2)
            cond_low(0, 3)
            router_low()
            for p in range(1, NP):
                v = W_Q + 3 * (p - 1)
                k_bias(0, p)
                if p < 3:
                    weight_low(v, v + 1)
                k_max(0, p)
                if p < 3:
                    weight_low(v + 1, v + 2)
                v_bias(0, p)
                if p < 3:
                    weight_low(v + 2, v + 3)
                kvprod_low(0, p - 1, FIRST)
            weight_low(10, W_O)
            kvprod_low(0, 3, FIRST)
            body_a(0, 0)
            with dve.Fori(1, NG - 1) as g:
                body_a(g, 0)
            body_a(NG - 1, 1)
            with dve.Fori(NG, 2 * NG - 1) as g:
                body_b(g, True)
            body_b(2 * NG - 1, False)

        @block.tensor
        def _(pe):
            pe.sem_inc(heads_free, A_CR)
            pe.sem_inc(o_free, 1)

            def product(out, lhs, rhs, k, n):
                for q, (a, b) in enumerate(PASSES):
                    last = nc.tensor.matmul(out, lhs(a), rhs(b), start=(k == 0 and q == 0),
                                            stop=(k == n - 1 and q == len(PASSES) - 1))
                return last

            def cond(g, p, f, order=STEADY):
                s = p % 2
                pe.wait_ge(x_lo, g * NP + p + 1)
                if order is STEADY:
                    pe.wait_ge(f_read, f + p - 1)
                elif p >= 2:
                    pe.wait_ge(f_read, bank_read(order, "cond", p))
                for k in range(KC):
                    last = product(F[s][:, k * 128:(k + 1) * 128], lambda a: xs[:, s, a, k * 128:(k + 1) * 128],
                                   lambda b: cws[:, s, b, :], 0, 1)
                last.then_inc(cond_done, 1)

            def project(g, p, n, f, order=STEADY):
                pe.wait_ge(f_read, f + max(read(order, "cond", p), bank_read(order, "kv"[n], p)))
                for k in range(KC):
                    last = product(F[n][:], lambda a: hT[:, a, k, p * 128:(p + 1) * 128],
                                   lambda b: (wk, wv)[n][:, b, k, :], k, KC)
                last.then_inc((k_done, v_done)[n], 1)

            def kv_product(g, p, n, f, order=STEADY):
                s, jj, b = p % 2, n // 2, n % 2
                if n == 0:
                    pe.wait_ge(sk_lo, g * NP + p + 1)
                    pe.wait_ge(vs_lo, g * NP + p + 1)
                before = bank_read(order, "kv", p, n)
                if before is not None:
                    pe.wait_ge(f_read, f + before)
                rows = slice(64 * b, 64 * b + 64)
                for t in range(2):
                    j = 2 * jj + t
                    last = product(bank(order, ("kv", p, n))[0][:, t * DV:(t + 1) * DV], lambda a: sk[rows, s, a, j * D:(j + 1) * D],
                                   lambda c: vs[rows, s, c, j, :], 0, 1)
                last.then_inc(kv_done, 1)

            def wide(g, h, w1=False):
                pe.wait_ge(q_free[h % 2], (SQ_ // 2) * g + h // 2 + 1)
                if h % 4 == 0:
                    if w1:
                        pe.wait_ge(st_lo, h // 2 + 2)
                    else:
                        pe.wait_ge(w_lo, W_Q + h // 2 + 2)
                for k in range(KC):
                    last = product(Q[h % 2][:], lambda a: wa[:, a, k, h * D:(h + 1) * D], lambda b: hT[:, b, k, :], k, KC)
                last.then_inc(q_done, 1)

            def heads(g, n):
                j, i = n // NP, n % NP
                pe.wait_ge(e_free, H * g + GQ * j + GQ - 1 + 3)
                pe.wait_ge(m_free, SA_ * g + n + 1)
                for b in range(2):
                    for t in range(2):
                        last = product(M[n % 2][:, b, t * DV:(t + 1) * DV],
                                       lambda a: sq[:, j % 2, a, 2 * i + b, t, :, :].rearrange("p s h -> p (s h)"),
                                       lambda c: kv[:, c, 2 * i + b, j, :], 0, 1)
                last.then_inc(heads_free, 1)

            def output(g, p, c, w2=False):
                if c == 0:
                    pe.wait_ge(q_free[p % 2], (SQ_ // 2) * g + H // 2 + p // 2 + 1)
                if not w2:
                    pe.wait_ge(w_lo, W_O + 2 * (c + 1))
                    n = NP * c + p
                    pe.wait_ge(turned[n % 2], 16 * (SA_ // 2) * g + 16 * (n // 2 + 1))
                elif p == 0:
                    pe.wait_ge(st_lo, S_1 + 2 * (c + 1))
                    pe.wait_ge(e_free, H * g + 4 * c + 3 + 3)
                for h in range(4 * c, 4 * c + 4):
                    last = product(Q[p % 2][:], lambda a: mid[:, a, h, p * 128:(p + 1) * 128] if w2 else
                                   mid_h[:, NP * c + p, a, h % GQ // 2, :, h % 2],
                                   lambda b: (w2s[b] if w2 else wb[:, b])[:, h, :], h, H)
                if c == 3:
                    last.then_inc(o_free, 1)

            def router(g):
                if not (isinstance(g, int) and g == NG):
                    pe.wait_ge(lg_read, g - NG)
                else:
                    pe.wait_ge(m_free, SA_ * NG + 2)
                for p in range(NP):
                    for k in range(KC):
                        last = product(M[0][:, 0, p * NB:(p + 1) * NB], lambda a: hT[:, a, k, p * 128:(p + 1) * 128],
                                       lambda b: wr[:, b, k, :], k, KC)
                last.then_inc(routed, 1)

            def turn_mask(g):
                pe.wait_ge(masked, g - NG + 1)
                if not (isinstance(g, int) and g == NG):
                    pe.wait_ge(maskT_sb, g - NG)
                for p in range(NP):
                    last = nc.tensor.transpose(M[0][0:NB, 1, p * 128:(p + 1) * 128], mask[:, p, :], ident[:])
                last.then_inc(maskT_ps, 1)

            BETWEEN = {(0, n): (1, n + 1) for n in range(3)}
            BETWEEN.update({(1, n): (2, n) for n in range(4)})
            BETWEEN.update({(2, 0): (3, 0), (2, 1): (3, 1), (2, 3): (3, 2), (3, 1): (3, 3)})

            def body_a(g, nxt, f):
                for h in range(H):
                    wide(g, h)
                    if h == 5:
                        pe.wait_ge(f_read, f)
                    if h >= 5:
                        heads(g, h - 5)
                    if h in (13, 14):
                        cond(g + 1, h - 13, f)
                output(g, 0, 0)
                heads(g, 11)
                output(g, 0, 1)
                heads(g, 12)
                cond(g + 1, 2, f)
                output(g, 0, 2)
                heads(g, 13)
                cond(g + 1, 3, f)
                output(g, 1, 0)
                if nxt == 0:
                    project(g + 1, 0, 0, f)
                    heads(g, 14)
                    project(g + 1, 0, 1, f)
                    heads(g, 15)
                    project(g + 1, 1, 0, f)
                    output(g, 0, 3)
                    project(g + 1, 1, 1, f)
                    for p in range(NP):
                        if 0 < p < 3:
                            project(g + 1, p + 1, 0, f)
                            project(g + 1, p + 1, 1, f)
                        for n in range(4):
                            kv_product(g + 1, p, n, f)
                            if (p, n) in BETWEEN:
                                output(g, *BETWEEN[p, n])
                else:
                    heads(g, 14)
                    output(g, 1, 1)
                    heads(g, 15)
                    output(g, 1, 2)
                    output(g, 0, 3)
                    output(g, 1, 3)
                    pe.wait_ge(f_read, f + NP)
                    router(g + 1)
                    for p in (2, 3):
                        for c in range(4):
                            output(g, p, c)
                        if p == 2:
                            turn_mask(g + 1)

            def body_b(g, more, f):
                for h in range(H):
                    wide(g, h, w1=True)
                    if more and h in (13, 14):
                        cond(g + 1, h - 13, f)
                for p in range(NP):
                    for c in range(4):
                        output(g, p, c, w2=True)
                        if more and p == 0 and c in (1, 2):
                            cond(g + 1, 1 + c, f)
                    if more and p == 0:
                        pe.wait_ge(f_read, f + NP)
                        router(g + 1)
                    if more and p == 1:
                        turn_mask(g + 1)

            def keep_warm(n):
                for _ in range(n):
                    nc.tensor.matmul(Q[1][:], zeros[:, 0:128], zeros, start=True, stop=True)

            pe.wait_ge(zeros_set, 1)
            keep_warm(18)
            cond(0, 0, 0, FIRST)
            cond(0, 1, 0, FIRST)
            keep_warm(15)
            pe.wait_ge(w_lo, 2)
            project(0, 0, 0, 0, FIRST)
            pe.wait_ge(w_lo, W_Q)
            project(0, 0, 1, 0, FIRST)
            cond(0, 2, 0, FIRST)
            cond(0, 3, 0, FIRST)
            keep_warm(10)
            pe.wait_ge(pool_consts, 4)
            pe.wait_ge(dve_consts, 5)
            for p in range(NP):
                if p + 1 < NP:
                    project(0, p + 1, 0, 0, FIRST)
                    project(0, p + 1, 1, 0, FIRST)
                if p == NP - 1:
                    keep_warm(7)
                for n in range(4):
                    kv_product(0, p, n, 0, FIRST)
            body_a(0, 0, SF_)
            with pe.Fori(1, NG - 1) as g:
                body_a(g, 0, (g + 1) * SF_)
            body_a(NG - 1, 1, SF_ * NG)
            with pe.Fori(NG, 2 * NG - 1) as g:
                body_b(g, True, SF_ * NG + NP * (g + 1 - NG))
            body_b(2 * NG - 1, False, None)


_SHAPE = (B, C, T)


def kernel(**inputs):
    import numpy as _np
    import concourse.bacc as _bacc
    from concourse import mybir as _mybir
    from concourse.bass_utils import run_bass_kernel_spmd as _run

    nc = _bacc.Bacc("TRN2", target_bir_lowering=False, num_devices=1)
    arr = {k: _np.asarray(v) for k, v in inputs.items()}
    laid = {
        "x": arr["x"], "i1": arr["itok_B_0_7"], "i2": arr["itok_B_1_198"],
        "cw": arr["L0_cond_weights"], "cw2": arr["L0_cond2_weights"],
        "wq": arr["L0_attn_Wq"].T, "wk": arr["L0_attn_Wk"].T, "wv": arr["L0_attn_Wv"].T, "wo": arr["L0_attn_Wo"].T,
        "bq": arr["L0_attn_bq"].reshape(H, D).T, "bk": arr["L0_attn_bk"], "bv": arr["L0_attn_bv"],
        "wr": arr["L0_ffn_Wr"].T, "br": arr["L0_ffn_br"], "w1": arr["L0_ffn_W1"].T, "w2": arr["L0_ffn_W2"].T,
    }
    arrays, args = {}, []
    for name, a in laid.items():
        a = _np.ascontiguousarray(a)
        arrays[f"in_{name}_dram"] = a
        args.append(nc.dram_tensor(f"in_{name}_dram", a.shape, _mybir.dt.from_np(a.dtype), kind="ExternalInput").ap())
    args.append(nc.dram_tensor("x1_dram", _SHAPE, _mybir.dt.float32, kind="Internal").ap())
    args.append(nc.dram_tensor("mask_dram", (NB, TOK), _mybir.dt.float16, kind="Internal").ap())
    args.append(nc.dram_tensor("out_0_dram", _SHAPE, _mybir.dt.float32, kind="ExternalOutput").ap())
    adaln_attn_ffn(nc, *args)
    r = _run(nc, [arrays], core_ids=[0])
    return r.results[0]["out_0_dram"]
```
